# Optimizing a Trainium2 kernel written in Bass

```python
import numpy as np
import jax
import jax.numpy as jnp

def _softmax(x, axis=-1):
    return jax.nn.softmax(x, axis=axis)

def _gelu(x):
    return jax.nn.gelu(x, approximate=True)

def _silu(x):
    return jax.nn.silu(x)

def _sigmoid(x):
    return jax.nn.sigmoid(x)

def _layernorm(x, axis=-1, eps=1e-05):
    m = jnp.mean(x, axis=axis, keepdims=True)
    v = jnp.var(x, axis=axis, keepdims=True)
    return (x - m) / jnp.sqrt(v + eps)

def _scatter_add(tgt, idx, src, axis=0):
    return tgt.at[idx].add(src)

def _segment_sum(src, seg, n):
    return jax.ops.segment_sum(src, seg, n)
kernel_name = 'mk_seq_postln_d1_jaxref_r4_e7b99e'

def setup_inputs(seed: int=0):
    np.random.seed(seed)
    _w = jnp.asarray

    def _L0_attn_setup():
        import jax, jax.numpy as jnp
        import numpy as np
        B, T, HID, H = (2, 512, 512, 16)
        D = HID // H

        def apply_rope(x):
            b, t, h, d = x.shape
            half = d // 2
            x1, x2 = (x[..., :half], x[..., half:])
            theta = 1.0 / 10000.0 ** (jnp.arange(0, half, 2, dtype=jnp.float32) / half)
            pos = jnp.arange(t, dtype=jnp.float32)
            freq = pos[:, None] * theta[None, :]
            sin = jnp.sin(freq)[None, :, None, :]
            cos = jnp.cos(freq)[None, :, None, :]
            x1e, x1o = (x1[..., ::2], x1[..., 1::2])
            x2e, x2o = (x2[..., ::2], x2[..., 1::2])
            x1r = jnp.concatenate([x1e * cos - x1o * sin, x1e * sin + x1o * cos], axis=-1)
            x2r = jnp.concatenate([x2e * cos - x2o * sin, x2e * sin + x2o * cos], axis=-1)
            return jnp.concatenate([x1r, x2r], axis=-1)
        key = jax.random.key(seed)
        ks = jax.random.split(key, 5)
        s = 0.02
        return {'hidden_states': jax.random.normal(ks[0], (B, T, HID), dtype=jnp.float32), 'Wq': jax.random.normal(ks[1], (HID, HID), dtype=jnp.float32) * s, 'Wk': jax.random.normal(ks[2], (D, HID), dtype=jnp.float32) * s, 'Wv': jax.random.normal(ks[3], (D, HID), dtype=jnp.float32) * s, 'Wo': jax.random.normal(ks[4], (HID, HID), dtype=jnp.float32) * s}
    _L0_attn_in = _L0_attn_setup()

    def _L0_ffn_setup():
        import jax, jax.numpy as jnp
        import numpy as np
        BS, SLEN, DIM, HID, E, TOPK = (4, 512, 512, 448, 8, 2)
        key = jax.random.key(seed)
        ks = jax.random.split(key, 9)
        s = 0.02
        return {'x': jax.random.normal(ks[0], (BS, SLEN, DIM), jnp.float32), 'gate_w': jax.random.normal(ks[1], (DIM, E), jnp.float32) * s, 'w1': jax.random.normal(ks[2], (E, DIM, HID), jnp.float32) * s, 'w2': jax.random.normal(ks[3], (E, HID, DIM), jnp.float32) * s, 'w3': jax.random.normal(ks[4], (E, DIM, HID), jnp.float32) * s, 'sw1': jax.random.normal(ks[5], (DIM, HID), jnp.float32) * s, 'sw2': jax.random.normal(ks[6], (HID, DIM), jnp.float32) * s, 'sw3': jax.random.normal(ks[7], (DIM, HID), jnp.float32) * s, 'expert_bias': jnp.zeros((E,), jnp.float32)}
    _L0_ffn_in = _L0_ffn_setup()
    _d = {'L0_attn_hidden_states': _L0_attn_in['hidden_states'], 'L0_attn_Wq': _L0_attn_in['Wq'], 'L0_attn_Wk': _L0_attn_in['Wk'], 'L0_attn_Wv': _L0_attn_in['Wv'], 'L0_attn_Wo': _L0_attn_in['Wo'], 'L0_ffn_gate_w': _L0_ffn_in['gate_w'], 'L0_ffn_w1': _L0_ffn_in['w1'], 'L0_ffn_w2': _L0_ffn_in['w2'], 'L0_ffn_w3': _L0_ffn_in['w3'], 'L0_ffn_sw1': _L0_ffn_in['sw1'], 'L0_ffn_sw2': _L0_ffn_in['sw2'], 'L0_ffn_sw3': _L0_ffn_in['sw3'], 'L0_ffn_expert_bias': _L0_ffn_in['expert_bias']}
    _x0 = _d['L0_attn_hidden_states']
    _d['L0_attn_hidden_states'] = jax.random.normal(jax.random.fold_in(jax.random.key(seed), 1), (4, 2048, 512), dtype=_x0.dtype)
    del _x0
    return _d

def reference(L0_attn_hidden_states, L0_attn_Wq, L0_attn_Wk, L0_attn_Wv, L0_attn_Wo, L0_ffn_gate_w, L0_ffn_w1, L0_ffn_w2, L0_ffn_w3, L0_ffn_sw1, L0_ffn_sw2, L0_ffn_sw3, L0_ffn_expert_bias):

    def _L0_attn_ref(hidden_states, Wq, Wk, Wv, Wo):
        import jax, jax.numpy as jnp
        import numpy as np
        B, T, HID, H = (2, 512, 512, 16)
        D = HID // H

        def apply_rope(x):
            b, t, h, d = x.shape
            half = d // 2
            x1, x2 = (x[..., :half], x[..., half:])
            theta = 1.0 / 10000.0 ** (jnp.arange(0, half, 2, dtype=jnp.float32) / half)
            pos = jnp.arange(t, dtype=jnp.float32)
            freq = pos[:, None] * theta[None, :]
            sin = jnp.sin(freq)[None, :, None, :]
            cos = jnp.cos(freq)[None, :, None, :]
            x1e, x1o = (x1[..., ::2], x1[..., 1::2])
            x2e, x2o = (x2[..., ::2], x2[..., 1::2])
            x1r = jnp.concatenate([x1e * cos - x1o * sin, x1e * sin + x1o * cos], axis=-1)
            x2r = jnp.concatenate([x2e * cos - x2o * sin, x2e * sin + x2o * cos], axis=-1)
            return jnp.concatenate([x1r, x2r], axis=-1)
        b, t, _ = hidden_states.shape
        scaling = D ** (-0.5)
        q = (hidden_states @ Wq.T).reshape(b, t, H, D).transpose(0, 2, 1, 3)
        k = hidden_states @ Wk.T
        v = hidden_states @ Wv.T
        q = apply_rope(q)
        k = apply_rope(k[:, None])
        v = v[:, None]
        scores = jnp.einsum('bhqd,bokd->bhqk', q, k) * scaling
        causal = jnp.tril(jnp.ones((t, t), dtype=bool))
        scores = jnp.where(causal[None, None], scores, -jnp.inf)
        probs = jax.nn.softmax(scores, axis=-1)
        attn = jnp.einsum('bhqk,bokd->bhqd', probs, v)
        attn = attn.transpose(0, 2, 1, 3).reshape(b, t, HID)
        return attn @ Wo.T

    def _L0_ffn_ref(x, gate_w, w1, w2, w3, sw1, sw2, sw3, expert_bias):
        import jax, jax.numpy as jnp
        import numpy as np
        BS, SLEN, DIM, HID, E, TOPK = (4, 512, 512, 448, 8, 2)
        bs, slen, dim = x.shape
        T = bs * slen
        xf = x.reshape(T, dim)
        scores = jax.nn.softmax((xf @ gate_w).astype(jnp.float32), axis=-1)
        _, sel = jax.lax.top_k(scores + expert_bias[None, :], TOPK)
        top_scores = jnp.take_along_axis(scores, sel, axis=1)
        flat_sel = sel.reshape(-1)
        counts = jnp.bincount(flat_sel, length=E).astype(jnp.int32)
        order = jnp.argsort(flat_sel, stable=True)
        top_scores_sorted = top_scores.reshape(-1)[order]
        token_idx = order // TOPK
        routed_in = xf[token_idx] * top_scores_sorted[:, None]
        h = jax.nn.silu(jax.lax.ragged_dot(routed_in, w1, counts)) * jax.lax.ragged_dot(routed_in, w3, counts)
        routed_out = jax.lax.ragged_dot(h, w2, counts)
        out = jax.nn.silu(xf @ sw1) * (xf @ sw3) @ sw2
        out = out.at[token_idx].add(routed_out)
        return out.reshape(bs, slen, dim)
    x = L0_attn_hidden_states
    x = _layernorm(x + _L0_attn_ref(x, L0_attn_Wq, L0_attn_Wk, L0_attn_Wv, L0_attn_Wo), axis=-1)
    x = _layernorm(x + _L0_ffn_ref(x, L0_ffn_gate_w, L0_ffn_w1, L0_ffn_w2, L0_ffn_w3, L0_ffn_sw1, L0_ffn_sw2, L0_ffn_sw3, L0_ffn_expert_bias), axis=-1)
    return x

_drawn_inputs = setup_inputs


def setup_inputs(seed=0):
    import zlib

    import numpy as np

    out = dict(_drawn_inputs(seed))
    spreads = {'L0_ffn_expert_bias': (0.0, 0.8)}
    factors = {'L0_attn_Wq': 8.0,
     'L0_attn_Wk': 8.0,
     'L0_attn_Wv': 4.205,
     'L0_attn_Wo': 4.159,
     'L0_ffn_gate_w': 8.0,
     'L0_ffn_w1': 8.0,
     'L0_ffn_w2': 8.0,
     'L0_ffn_w3': 8.0}
    for name, (base, spread) in spreads.items():
        noise = np.random.default_rng([zlib.crc32(name.encode()), seed]).standard_normal(out[name].shape)
        drawn = base * np.exp(spread * noise) if base else spread * noise
        out[name] = jnp.asarray(drawn.astype(out[name].dtype))
    for name, factor in factors.items():
        out[name] = (out[name] * factor).astype(out[name].dtype)
    return out
```

```python
import concourse.bass as bass
from concourse import mybir
from contextlib import ExitStack


def build(nc, B, T, HID, H, F, NE, TOPK,
          x, x_t, wq_t, wk_t, wv_t, wo_t, rope_cos, rope_sin, gate_w, expert_bias, w_all,
          c_expert, c_token, c_tile, c_tri, out):
    f32, f32r, bf16, i32 = mybir.dt.float32, mybir.dt.float32r, mybir.dt.bfloat16, mybir.dt.int32
    ALU, ACT, AX = mybir.AluOpType, mybir.ActivationFunctionType, mybir.AxisListType
    ds = bass.ds

    P, PLOG = 128, 7
    N = B * T
    D = HID // H
    KC = HID // P
    HG = P // D
    NG = H // HG
    CH = 512
    NCH = N // CH
    QT = T // P
    NU = B * NG
    NT = N // P
    RT = TOPK * NT + NE
    FP = F // KC
    W3, W2, WW = KC * F, 2 * KC * F, 2 * KC * F + KC * HID
    SCALE = float(D) ** -0.5
    MASKED = -1e30
    EPS = 1e-5
    SPLIT = 1584
    NSPLIT = (NE + 1) * WW // SPLIT
    VW = D + 1
    SR = 3 * D
    assert NSPLIT % (2 * NU) == 0 or NSPLIT % NU == 0
    assert NSPLIT * SPLIT == (NE + 1) * WW

    def dram(name, shape, dt):
        return nc.dram_tensor(name, shape, dt).ap()

    q_dram = dram("q_dram", (2, NG, HG, D, N), f32)
    k_dram = dram("k_dram", (SR + 1, N), f32)
    v_dram = dram("v_dram", (P, NT, VW), f32)
    w_dram = dram("w_dram", (2, P, (NE + 1) * WW), f32)
    attn_dram = dram("attn_dram", (N, HID), f32)
    x1_dram = dram("x1_dram", (N, HID), f32)
    y_dram = dram("y_dram", (N, HID), f32)
    r_dram = dram("r_dram", (RT * P, HID), f32)
    list_dram = dram("list_dram", (P * RT, 2), i32)

    top = ExitStack()

    def sem(stack, name):
        return stack.enter_context(nc.semaphore(name))

    def sb(stack, name, shape, dt=f32):
        return stack.enter_context(nc.sbuf_tensor(name, shape, dt))

    def wait_alone(eng, s, value):
        eng.wait_ge(s, value)
        eng.sem_inc(s_passed, 1)

    s_passed = sem(top, "s_passed")
    psum = top.enter_context(nc.psum_tensor("psum", [P, 8, 512], f32))
    ident = sb(top, "ident", [P, P])
    identb = sb(top, "identb", [P, P], bf16)
    mask_q = sb(top, "mask_q", [P, P], bf16)
    mask_k = sb(top, "mask_k", [P, HG, P], bf16)
    logits = sb(top, "logits", [P, NT, NE])
    pos = sb(top, "pos", [P, TOPK, NT], i32)

    def projections():
        with ExitStack() as st:
            xt = sb(st, "xt", [P, 2, KC, CH])
            wq = sb(st, "wq", [P, KC, H, 2, D // 2])
            wqr = sb(st, "wqr", [P, KC, H, 2, D // 2])
            wk = sb(st, "wk", [P, KC, SR])
            wv = sb(st, "wv", [P, KC, D])
            cos = sb(st, "cos", [P, H, D // 2])
            sin = sb(st, "sin", [P, H, D // 2])
            t1 = sb(st, "t1", [P, 2, H, D // 2])
            kst = sb(st, "kst", [SR + 1, 2, CH], f32r)
            vst = sb(st, "vst", [P, 2, CH // P, VW])
            qhi = sb(st, "qhi", [P, 2, CH], f32r)
            qlo = sb(st, "qlo", [P, 2, CH], f32r)
            s_w, s_rot, s_step = sem(st, "s1_w"), sem(st, "s1_rot"), sem(st, "s1_step")
            s_x = [sem(st, f"s1_x{r}") for r in range(2)]
            s_used, s_mm, s_ev, s_hi = sem(st, "s1_used"), sem(st, "s1_mm"), sem(st, "s1_ev"), sem(st, "s1_hi")
            s_init, s_k, s_wkv = sem(st, "s1_init"), sem(st, "s1_k"), sem(st, "s1_wkv")
            s_kv = [sem(st, f"s1_kv{r}") for r in range(2)]
            s_q = [sem(st, f"s1_q{r}") for r in range(2)]
            s_list = sem(st, "s1_list")
            zero = sb(st, "zero", [P, 2 * RT], i32)
            UN = 2 + NG
            block = st.enter_context(nc.Block())

            @block.sync
            def _(sp):
                sp.dma_start(wq[:, :, :, :, :].rearrange("p c h e d -> p c (h e d)"),
                             wq_t.rearrange("(c p) n -> p c n", p=P)).then_inc(s_w, 16)
                sp.dma_start(cos[:, :, :], rope_cos).then_inc(s_w, 16)
                sp.dma_start(sin[:, :, :], rope_sin).then_inc(s_w, 16)
                sp.dma_start(wk[:, :, :], wk_t.rearrange("(c p) n -> p c n", p=P)).then_inc(s_wkv, 16)
                sp.dma_start(wv[:, :, :], wv_t.rearrange("(c p) n -> p c n", p=P)).then_inc(s_wkv, 16)
                sp.sem_inc(s_kv[0], 32)
                sp.sem_inc(s_kv[1], 32)
                sp.sem_inc(s_q[0], 32)
                sp.sem_inc(s_q[1], 32)
                with sp.Fori(0, NCH // 2) as i:
                    for r in range(2):
                        c = 2 * i + r
                        sp.wait_ge(s_ev, UN * c + UN + 2)
                        sp.dma_start(k_dram[:, ds(c * CH, CH)], kst[:, r, :].bitcast(f32)).then_inc(s_kv[r], 16)
                        sp.dma_start(v_dram[:, ds(c * (CH // P), CH // P), :],
                                       vst[:, r, :, :]).then_inc(s_kv[r], 16)
                        for g in range(NG):
                            sp.wait_ge(s_ev, UN * c + UN + 3 + g)
                            for part, src in ((0, qhi), (1, qlo)):
                                dst = q_dram[part, g].rearrange("j d n -> (j d) n")
                                sp.dma_start(dst[:, ds(c * CH, CH)], src[:, g % 2, :].bitcast(f32)).then_inc(s_q[g % 2], 16)
                for r in range(2):
                    sp.wait_ge(s_kv[r], 32 + 32 * (NCH // 2))
                    sp.wait_ge(s_q[r], 32 + 32 * NCH * (NG // 2))

            @block.gpsimd
            def _(pool):
                pool.memset(ident[:, :], 0.0).then_inc(s_init, 1)
                pool.memset(mask_q[:, :], 0.0).then_inc(s_init, 1)
                pool.memset(mask_k[:, :, :], 0.0).then_inc(s_init, 1)
                pool.memset(zero[:, :], 0).then_inc(s_init, 1)
                wait_alone(pool, s_init, 4)
                pool.affine_select(out=ident[:, :], in_=ident[:, :], compare_op=ALU.not_equal, fill=1.0,
                                   base=0, pattern=[[-1, P]], channel_multiplier=1).then_inc(s_init, 1)
                pool.affine_select(out=mask_q[:, :], in_=mask_q[:, :], compare_op=ALU.is_ge, fill=MASKED,
                                   base=0, pattern=[[-1, P]], channel_multiplier=1).then_inc(s_init, 1)
                pool.affine_select(out=mask_k[:, :, :], in_=mask_k[:, :, :], compare_op=ALU.is_ge, fill=MASKED,
                                   base=0, pattern=[[0, HG], [1, P]], channel_multiplier=-1).then_inc(s_init, 1)
                wait_alone(pool, s_init, 7)
                pool.tensor_copy(identb[:, :], ident[:, :]).then_inc(s_init, 1)
                pool.dma_start(list_dram.rearrange("(p t) e -> p (t e)", p=P), zero[:, :]).then_inc(s_list, 16)
                x_cols = x_t.rearrange("(c p) n -> p c n", p=P)
                with pool.Fori(0, NCH // 2) as i:
                    for r in range(2):
                        c = 2 * i + r
                        wait_alone(pool, s_used, c + 1)
                        pool.dma_start(xt[:, r, :, :], x_cols[:, :, ds(c * CH, CH)]).then_inc(s_x[r], 16)
                wait_alone(pool, s_list, 16)

            @block.tensor
            def _(pe):
                pe.sem_inc(s_used, 2)
                pe.wait_ge(s_wkv, 32)
                pe.wait_ge(s_rot, 1)
                with pe.Fori(0, NCH // 2) as i:
                    for r in range(2):
                        c = 2 * i + r
                        pe.wait_ge(s_x[r], 16 * i + 16)
                        for n in range(UN):
                            pe.wait_ge(s_ev, UN * c + n + 1)
                            if n == 0:
                                for k in range(KC):
                                    mm = nc.tensor.matmul(psum[0:SR, n, :], wk[:, k, :], xt[:, r, k, :],
                                                          start=(k == 0), stop=(k == KC - 1))
                            elif n == 1:
                                for j in range(CH // P):
                                    for k in range(KC):
                                        mm = nc.tensor.matmul(psum[:, n, j * D:(j + 1) * D],
                                                              xt[:, r, k, j * P:(j + 1) * P], wv[:, k, :],
                                                              start=(k == 0), stop=(k == KC - 1))
                            else:
                                heads = slice((n - 2) * HG, (n - 1) * HG)
                                for k in range(KC):
                                    mm = nc.tensor.matmul(psum[:, n, :], wqr[:, k, heads, :, :],
                                                          xt[:, r, k, :], start=(k == 0), stop=(k == KC - 1))
                            mm.then_inc(s_mm, 1)
                        pe.wait_ge(s_mm, UN * c + UN)
                        pe.sem_inc(s_used, 1)

            @block.vector
            def _(dve):
                dve.sem_inc(s_ev, UN)
                dve.wait_ge(s_w, 48)
                for k in range(KC):
                    a, b = wq[:, k, :, 0, :], wq[:, k, :, 1, :]
                    for half, (first, second, op) in enumerate(((cos, sin, ALU.subtract), (sin, cos, ALU.add))):
                        n = 2 * k + half
                        if n >= 1:
                            dve.wait_ge(s_step, 3 * n)
                        nc.vector.tensor_tensor(t1[:, 0], a, first[:, :, :], ALU.mult).then_inc(s_step, 1)
                        nc.vector.tensor_tensor(t1[:, 1], b, second[:, :, :], ALU.mult).then_inc(s_step, 1)
                        dve.wait_ge(s_step, 3 * n + 2)
                        nc.vector.tensor_tensor(wqr[:, k, :, half, :], t1[:, 0], t1[:, 1], op).then_inc(s_step, 1)
                dve.wait_ge(s_step, 6 * KC)
                dve.sem_inc(s_rot, 1)
                nc.vector.memset(kst[SR:SR + 1, :, :].bitcast(f32), 1.0).then_inc(s_k, 1)
                nc.vector.memset(vst[:, :, :, D:VW], 1.0).then_inc(s_k, 1)
                dve.wait_ge(s_k, 2)
                with dve.Fori(0, NCH // 2) as i:
                    for r in range(2):
                        c = 2 * i + r
                        dve.wait_ge(s_kv[r], 32 * i + 32)
                        dve.wait_ge(s_mm, UN * c + 1)
                        nc.vector.tensor_copy(kst[0:SR, r, :], psum[0:SR, 0, :]).then_inc(s_k, 1)
                        dve.wait_ge(s_k, c + 3)
                        nc.vector.tensor_tensor(kst[2 * D:SR, r, :], psum[2 * D:SR, 0, :],
                                                kst[2 * D:SR, r, :].bitcast(f32), ALU.subtract).then_inc(s_ev, 1)
                        dve.wait_ge(s_mm, UN * c + 2)
                        nc.vector.tensor_copy(vst[:, r, :, 0:D],
                                              psum[:, 1, 0:CH // P * D].rearrange("p (j d) -> p j d", d=D)
                                              ).then_inc(s_ev, 1)
                        for g in range(NG):
                            dve.wait_ge(s_hi, NG * c + g + 1)
                            nc.vector.tensor_tensor(qlo[:, g % 2, :], psum[:, 2 + g, :],
                                                    qhi[:, g % 2, :].bitcast(f32), ALU.subtract).then_inc(s_ev, 1)

            @block.scalar
            def _(act):
                with act.Fori(0, NCH // 2) as i:
                    for r in range(2):
                        c = 2 * i + r
                        for g in range(NG):
                            act.wait_ge(s_mm, UN * c + 3 + g)
                            act.wait_ge(s_q[g % 2], 32 * (NG // 2) * c + 32 * (g // 2) + 32)
                            nc.scalar.activation(qhi[:, g % 2, :], psum[:, 2 + g, :], ACT.Copy).then_inc(s_hi, 1)

    def attention():
        steps = [(q, s, 2 * s, min(2, q + 1 - 2 * s)) for q in range(QT) for s in range((q + 2) // 2)]
        last_step = {q: max(g for g, t in enumerate(steps) if t[0] == q) for q in range(QT)}
        NS = len(steps)

        def max_units(q):
            return [("max", q, h, c) for h in range(HG) for c in range((q * P + P + CH - 1) // CH)]

        ahead = max_units(0) + [("shift", 0)] + (max_units(1) if QT > 1 else [])
        after = []
        for g, (q, s, _, _) in enumerate(steps):
            ns = (q + 2) // 2
            todo = max_units(q + 2) if q + 2 < QT else []
            side = []
            if s == min(1, ns - 1) and q + 1 < QT:
                side.append(("shift", q + 1))
            side += todo[len(todo) * s // ns:len(todo) * (s + 1) // ns]
            if s == ns - 1 and q >= 1:
                side.append(("turn", q - 1))
            after.append(side)
        tail = [("turn", QT - 1)]
        order = ahead + [e for side in after for e in side] + tail
        NA = len(order)
        index = {e: n for n, e in enumerate(order)}
        assert NA % 2 == 0 and NS % 6 == 0, (NA, NS)

        with ExitStack() as st:
            qs = [sb(st, f"qs{r}", [SR + 1, HG, T], f32r) for r in range(2)]
            ks = [sb(st, f"ks{r}", [SR + 1, T], f32r) for r in range(2)]
            vs = [sb(st, f"vs{r}", [P, QT, VW]) for r in range(2)]
            probs = sb(st, "probs", [P, 3, 2, HG * P])
            o_t = sb(st, "o_t", [VW, 2, HG * P])
            attn = [sb(st, f"attn{r}", [P, QT, HG, D]) for r in range(2)]
            mparts = sb(st, "mparts", [P, 2, HG, T // CH])
            mfull = sb(st, "mfull", [P, 2, HG])
            mrow = sb(st, "mrow", [HG, 2, P], f32r)
            rden = sb(st, "rden", [P, 2, HG])
            raw = sb(st, "raw", [P, 2, SPLIT])
            whi = sb(st, "whi", [P, 2, SPLIT], f32r)
            wlo = sb(st, "wlo", [P, 2, SPLIT], f32r)
            s_ld = [sem(st, f"s2_ld{r}") for r in range(2)]
            s_unit, s_side, s_read = sem(st, "s2_unit"), sem(st, "s2_side"), sem(st, "s2_read")
            s_sc, s_pr, s_pv, s_oc = sem(st, "s2_sc"), sem(st, "s2_pr"), sem(st, "s2_pv"), sem(st, "s2_oc")
            s_mp, s_mf, s_row, s_rd = sem(st, "s2_mp"), sem(st, "s2_mf"), sem(st, "s2_row"), sem(st, "s2_rd")
            s_at = [sem(st, f"s2_at{r}") for r in range(2)]
            s_wl, s_ws, s_wst = sem(st, "s2_wl"), sem(st, "s2_ws"), sem(st, "s2_wst")
            block = st.enter_context(nc.Block())
            score_banks = lambda g: 2 + 2 * (g % 2)
            out_bank = lambda q: 6 + q % 2

            def units(eng, body):
                with eng.Fori(0, B) as b:
                    with eng.Fori(0, NG // 2) as gp:
                        for r in range(2):
                            body(b * NG + 2 * gp + r, b * (NG // 2) + gp, b, 2 * gp + r, r)

            @block.gpsimd
            def _(pool):
                WPU = NSPLIT // NU

                def unit(u, i, b, g, r):
                    wait_alone(pool, s_unit, u + 1)
                    pool.dma_start(ks[r][:, :].bitcast(f32), k_dram[:, ds(b * T, T)]).then_inc(s_ld[r], 16)
                    for row, part in ((0, 0), (D, 1), (2 * D, 0)):
                        src = q_dram[part].rearrange("g j d n -> d g j n")[:, ds(g, 1), :, ds(b * T, T)]
                        pool.dma_start(qs[r][row:row + D, :, :].bitcast(f32), src.rearrange("d g j n -> d (g j) n")
                                       ).then_inc(s_ld[r], 16)
                    pool.dma_start(vs[r][:, :, :], v_dram[:, ds(b * QT, QT), :]).then_inc(s_ld[r], 16)
                    for m in range(WPU):
                        n = u * WPU + m
                        pool.dma_start(raw[:, 0, :], w_all[:, ds(n * SPLIT, SPLIT)]).then_inc(s_wl, 16)
                        wait_alone(pool, s_wl, 16 * n + 16)
                        pool.tensor_copy(whi[:, 0, :], raw[:, 0, :]).then_inc(s_ws, 1)
                        wait_alone(pool, s_ws, 2 * n + 1)
                        pool.tensor_tensor(wlo[:, 0, :], raw[:, 0, :], whi[:, 0, :].bitcast(f32),
                                           ALU.subtract).then_inc(s_ws, 1)
                        wait_alone(pool, s_ws, 2 * n + 2)
                        pool.dma_start(w_dram[0, :, ds(n * SPLIT, SPLIT)], whi[:, 0, :].bitcast(f32)).then_inc(s_wst, 16)
                        pool.dma_start(w_dram[1, :, ds(n * SPLIT, SPLIT)], wlo[:, 0, :].bitcast(f32)).then_inc(s_wst, 16)
                        wait_alone(pool, s_wst, 32 * n + 32)

                units(pool, unit)

            @block.sync
            def _(sp):
                attn_rows = attn_dram.rearrange("(t p) n -> p t n", p=P)

                def unit(u, i, b, g, r):
                    for q in range(QT):
                        sp.wait_ge(s_read, u * NA + index[("shift", q)] + 3)
                        sp.dma_start(qs[r][SR:SR + 1, :, q * P:(q + 1) * P].bitcast(f32), mrow[:, q % 2, :].bitcast(f32)).then_inc(s_row, 16)
                    sp.wait_ge(s_read, u * NA + NA + 2)
                    sp.dma_start(attn_rows[:, ds(b * QT, QT), ds(g * P, P)],
                                 attn[r][:, :, :, :].rearrange("p t j d -> p t (j d)")).then_inc(s_at[r], 16)

                sp.sem_inc(s_at[0], 16)
                sp.sem_inc(s_at[1], 16)
                units(sp, unit)
                for r in range(2):
                    sp.wait_ge(s_at[r], 16 + 16 * (NU // 2))

            @block.tensor
            def _(pe):
                def side(u, r, e):
                    n = index[e]
                    bank = n % 2
                    pe.wait_ge(s_read, u * NA + n + 1)
                    if e[0] == "max":
                        _, q, h, c = e
                        w = min(CH, q * P + P - c * CH)
                        diag = c * CH + w == q * P + P
                        mm = nc.tensor.matmul(psum[:, bank, 0:w], qs[r][0:SR, h, q * P:(q + 1) * P],
                                              ks[r][0:SR, c * CH:c * CH + w], start=True, stop=not diag)
                        if diag:
                            mm = nc.tensor.matmul(psum[:, bank, w - P:w], identb[:, :], mask_q[:, :],
                                                  start=False, stop=True)
                    elif e[0] == "shift":
                        q = e[1]
                        pe.wait_ge(s_mf, u * QT + q + 1)
                        mm = nc.tensor.transpose(psum[0:HG, bank, 0:P], mfull[:, q % 2, :], ident[:, :])
                    else:
                        q = e[1]
                        wait_alone(pe, s_oc, u * QT + q + 3)
                        for h in range(HG):
                            mm = nc.tensor.transpose(psum[:, bank, h * VW:(h + 1) * VW],
                                                     o_t[:, q % 2, h * P:(h + 1) * P], ident[0:VW, 0:VW])
                    mm.then_inc(s_side, 1)

                def scores(u, r, g):
                    q, s, j0, nj = steps[g]
                    if s == 0:
                        pe.wait_ge(s_row, 16 * QT * u + 16 * q + 16)
                    pe.wait_ge(s_pr, u * NS + g + 1)
                    for jj in range(nj):
                        j = j0 + jj
                        o = psum[:, score_banks(g) + jj, :]
                        mm = nc.tensor.matmul(o, ks[r][:, j * P:(j + 1) * P], qs[r][:, :, q * P:(q + 1) * P],
                                              start=True, stop=(j != q))
                        if j == q:
                            mm = nc.tensor.matmul(o, identb[:, :], mask_k[:, :, :], start=False, stop=True)
                    mm.then_inc(s_sc, 1)

                def values(u, r, g):
                    q, s, j0, nj = steps[g]
                    pe.wait_ge(s_pr, u * NS + g + 3)
                    if s == 0:
                        pe.wait_ge(s_oc, u * QT + q + 1)
                    for jj in range(nj):
                        j = j0 + jj
                        mm = nc.tensor.matmul(psum[0:VW, out_bank(q), :], vs[r][:, j, :], probs[:, g % 3, jj, :],
                                              start=(j == 0), stop=(j == q))
                    mm.then_inc(s_pv, 1)

                def unit(u, i, b, g_, r):
                    pe.wait_ge(s_ld[r], 80 * i + 80)
                    for e in ahead:
                        side(u, r, e)
                    for g in range(NS):
                        scores(u, r, g)
                        if g >= 1:
                            values(u, r, g - 1)
                        for e in after[g]:
                            side(u, r, e)
                    values(u, r, NS - 1)
                    for e in tail:
                        side(u, r, e)
                    pe.wait_ge(s_side, u * NA + 2 * NA)
                    pe.sem_inc(s_unit, 1)

                pe.sem_inc(s_unit, 2)
                units(pe, unit)

            @block.scalar
            def _(act):
                def copy_out(u, q):
                    act.wait_ge(s_pv, u * NS + last_step[q] + 4)
                    n = index[("turn", q - 2)] + NA if q >= 2 else index[("turn", QT - 2 + q)]
                    act.wait_ge(s_side, u * NA + n + 1)
                    nc.scalar.activation(o_t[:, q % 2, :], psum[0:VW, out_bank(q), :], ACT.Copy).then_inc(s_oc, 1)

                def unit(u, i, b, g_, r):
                    for g, (q, s, j0, nj) in enumerate(steps):
                        act.wait_ge(s_sc, u * NS + g + 1)
                        act.wait_ge(s_pv, u * NS + g + 1)
                        nc.scalar.activation(probs[:, g % 3, 0:nj, :],
                                             psum[:, score_banks(g):score_banks(g) + nj, :],
                                             ACT.Exp, scale=SCALE).then_inc(s_pr, 1)
                        if g >= 1 and last_step[steps[g - 1][0]] == g - 1:
                            copy_out(u, steps[g - 1][0])
                    copy_out(u, QT - 1)

                act.sem_inc(s_pr, 2)
                act.sem_inc(s_pv, 3)
                act.sem_inc(s_oc, 2)
                act.sem_inc(s_side, NA)
                units(act, unit)

            @block.vector
            def _(dve):
                def side(u, i, r, e):
                    n = index[e]
                    bank = n % 2
                    dve.wait_ge(s_side, u * NA + NA + n + 1)
                    if e[0] == "max":
                        _, q, h, c = e
                        w = min(CH, q * P + P - c * CH)
                        nc.vector.reduce_max(mparts[:, q % 2, h, c:c + 1], psum[:, bank, 0:w], axis=AX.X
                                             ).then_inc(s_read, 1)
                        nchunk = (q * P + P + CH - 1) // CH
                        if h == HG - 1 and c == nchunk - 1:
                            dve.wait_ge(s_read, u * NA + n + 3)
                            nc.vector.reduce_max(mfull[:, q % 2, :], mparts[:, q % 2, :, 0:nchunk], axis=AX.X
                                                 ).then_inc(s_mf, 1)
                    elif e[0] == "shift":
                        q = e[1]
                        nc.vector.tensor_scalar(mrow[:, q % 2, :], psum[0:HG, bank, 0:P], -1.0, None, ALU.mult
                                                ).then_inc(s_read, 1)
                    else:
                        q = e[1]
                        if q == 0:
                            dve.wait_ge(s_at[r], 16 * i + 16)
                        turned = psum[:, bank, 0:HG * VW].rearrange("p (h v) -> p h v", v=VW)
                        nc.vector.reciprocal(rden[:, q % 2, :].rearrange("p (h o) -> p h o", o=1), turned[:, :, D:VW]
                                             ).then_inc(s_rd, 1)
                        dve.wait_ge(s_rd, u * QT + q + 1)
                        nc.vector.tensor_tensor(attn[r][:, q, :, :], turned[:, :, 0:D],
                                                rden[:, q % 2, :].rearrange("p (h o) -> p h o", o=1).to_broadcast([P, HG, D]),
                                                ALU.mult).then_inc(s_read, 1)

                def unit(u, i, b, g_, r):
                    for e in order:
                        side(u, i, r, e)

                dve.sem_inc(s_read, 2)
                units(dve, unit)

    def post_attention():
        with ExitStack() as st:
            wo = sb(st, "wo", [P, KC, HID])
            gw = sb(st, "gw", [P, KC, NE])
            at = sb(st, "at3", [P, 2, HID])
            xs = sb(st, "xs3", [P, 2, HID])
            att = sb(st, "att3", [P, 2, KC, P])
            xt = sb(st, "xt3", [P, 2, KC, P])
            y = sb(st, "y3", [P, 2, HID])
            x1 = sb(st, "x13", [P, 2, HID])
            stats = sb(st, "stats3", [P, 2, 6])
            mv = sb(st, "mv3", [P, 2, 2])
            std = sb(st, "std3", [P, 2])
            rstd = sb(st, "rstd3", [P, 2])
            s_w = sem(st, "s3_w")
            s_ld = [sem(st, f"s3_ld{r}") for r in range(2)]
            s_st = [sem(st, f"s3_st{r}") for r in range(2)]
            s_ta, s_ac, s_pr, s_y = sem(st, "s3_ta"), sem(st, "s3_ac"), sem(st, "s3_pr"), sem(st, "s3_y")
            s_x1, s_tx, s_xc, s_g, s_gc = (sem(st, "s3_x1"), sem(st, "s3_tx"), sem(st, "s3_xc"), sem(st, "s3_g"),
                                           sem(st, "s3_gc"))
            s_ln, s_var, s_std = sem(st, "s3_ln"), sem(st, "s3_var"), sem(st, "s3_std")
            block = st.enter_context(nc.Block())

            @block.sync
            def _(sp):
                sp.dma_start(wo[:, :, :], wo_t.rearrange("(c p) n -> p c n", p=P)).then_inc(s_w, 16)
                sp.dma_start(gw[:, :, :], gate_w.rearrange("(c p) n -> p c n", p=P)).then_inc(s_w, 16)
                sp.sem_inc(s_st[0], 16)
                sp.sem_inc(s_st[1], 16)
                with sp.Fori(0, NT // 2) as i:
                    for r in range(2):
                        t = 2 * i + r
                        sp.wait_ge(s_x1, t + 1)
                        sp.dma_start(x1_dram[ds(t * P, P), :], x1[:, r, :]).then_inc(s_st[r], 16)
                for r in range(2):
                    sp.wait_ge(s_st[r], 16 + 16 * (NT // 2))

            @block.gpsimd
            def _(pool):
                with pool.Fori(0, NT // 2) as i:
                    for r in range(2):
                        t = 2 * i + r
                        wait_alone(pool, s_y, t + 1)
                        pool.dma_start(at[:, r, :], attn_dram[ds(t * P, P), :]).then_inc(s_ld[r], 16)
                        pool.dma_start(xs[:, r, :], x[ds(t * P, P), :]).then_inc(s_ld[r], 16)

            @block.tensor
            def _(pe):
                def project(t, i, r):
                    pe.wait_ge(s_ld[r], 32 * i + 32)
                    pe.wait_ge(s_ac, t + 1)
                    for k in range(KC):
                        mm = nc.tensor.transpose(psum[:, 0, k * P:(k + 1) * P], at[:, r, k * P:(k + 1) * P], ident[:, :])
                    mm.then_inc(s_ta, 1)
                    pe.wait_ge(s_ac, t + 2)
                    pe.wait_ge(s_y, t + 2)
                    for k in range(KC):
                        mm = nc.tensor.matmul(psum[:, 1, :], att[:, r, k, :], wo[:, k, :],
                                              start=(k == 0), stop=(k == KC - 1))
                    mm.then_inc(s_pr, 1)

                def gate(t, i, r):
                    pe.wait_ge(s_x1, t + 1)
                    pe.wait_ge(s_xc, t + 1)
                    for k in range(KC):
                        mm = nc.tensor.transpose(psum[:, 2, k * P:(k + 1) * P], x1[:, r, k * P:(k + 1) * P], ident[:, :])
                    mm.then_inc(s_tx, 1)
                    pe.wait_ge(s_xc, t + 2)
                    pe.wait_ge(s_gc, t + 1)
                    for k in range(KC):
                        mm = nc.tensor.matmul(psum[:, 3, 0:NE], xt[:, r, k, :], gw[:, k, :],
                                              start=(k == 0), stop=(k == KC - 1))
                    mm.then_inc(s_g, 1)

                pe.wait_ge(s_w, 32)
                project(0, 0, 0)
                with pe.Fori(0, NT // 2 - 1) as i:
                    for r in range(2):
                        t = 2 * i + r
                        project(t + 1, i + r, 1 - r)
                        gate(t, i, r)
                project(NT - 1, NT // 2 - 1, 1)
                gate(NT - 2, NT // 2 - 1, 0)
                gate(NT - 1, NT // 2 - 1, 1)

            @block.scalar
            def _(act):
                def copy_attention(t, r):
                    act.wait_ge(s_ta, t + 1)
                    nc.scalar.activation(att[:, r, :, :].rearrange("p c n -> p (c n)"), psum[:, 0, :], ACT.Copy
                                         ).then_inc(s_ac, 1)

                def copy_x1(t, r):
                    act.wait_ge(s_tx, t + 1)
                    nc.scalar.activation(xt[:, r, :, :].rearrange("p c n -> p (c n)"), psum[:, 2, :], ACT.Copy
                                         ).then_inc(s_xc, 1)

                def root(t, r):
                    act.wait_ge(s_var, t + 1)
                    nc.scalar.activation(std[:, r:r + 1], mv[:, r, 1:2], ACT.Sqrt).then_inc(s_std, 1)

                act.sem_inc(s_ac, 1)
                act.sem_inc(s_xc, 1)
                copy_attention(0, 0)
                root(0, 0)
                with act.Fori(0, NT // 2 - 1) as i:
                    for r in range(2):
                        t = 2 * i + r
                        copy_attention(t + 1, 1 - r)
                        copy_x1(t, r)
                        root(t + 1, 1 - r)
                copy_attention(NT - 1, 1)
                copy_x1(NT - 2, 0)
                root(NT - 1, 1)
                copy_x1(NT - 1, 1)

            @block.vector
            def _(dve):
                def norm(t, i, r):
                    dve.wait_ge(s_pr, t + 1)
                    nc.vector.tensor_tensor(y[:, r, :], psum[:, 1, :], xs[:, r, :], ALU.add).then_inc(s_y, 1)
                    dve.wait_ge(s_y, t + 3)
                    nc.vector.bn_stats(stats[:, r, :], y[:, r, :]).then_inc(s_ln, 1)
                    wait_alone(dve, s_ln, 3 * t + 1)
                    nc.vector.bn_aggr(mv[:, r, :], stats[:, r, :]).then_inc(s_ln, 1)
                    dve.wait_ge(s_ln, 3 * t + 2)
                    nc.vector.tensor_scalar(mv[:, r, 1:2], mv[:, r, 1:2], EPS, None, ALU.add).then_inc(s_var, 1)
                    dve.wait_ge(s_std, t + 1)
                    nc.vector.reciprocal(rstd[:, r:r + 1], std[:, r:r + 1]).then_inc(s_ln, 1)
                    dve.wait_ge(s_ln, 3 * t + 3)
                    dve.wait_ge(s_st[r], 16 * i + 16)
                    nc.vector.tensor_scalar(x1[:, r, :], y[:, r, :], mv[:, r, 0:1], rstd[:, r:r + 1],
                                            ALU.subtract, ALU.mult).then_inc(s_x1, 1)

                def keep_logits(t):
                    dve.wait_ge(s_g, t + 1)
                    nc.vector.tensor_copy(logits[:, ds(t, 1), :].rearrange("p t e -> p (t e)"),
                                          psum[:, 3, 0:NE]).then_inc(s_gc, 1)

                dve.sem_inc(s_y, 2)
                dve.sem_inc(s_gc, 1)
                norm(0, 0, 0)
                with dve.Fori(0, NT // 2 - 1) as i:
                    for r in range(2):
                        t = 2 * i + r
                        norm(t + 1, i + r, 1 - r)
                        keep_logits(t)
                norm(NT - 1, NT // 2 - 1, 1)
                keep_logits(NT - 2)
                keep_logits(NT - 1)

    def expert_tiles(st, name, n_tiles, shared, block, xin, ybuf, score_of, weights_of, s_ld, s_used, s_y, s_st,
                     residual=None):
        xh = sb(st, name + "_xh", [P, KC, P], f32r)
        xl = sb(st, name + "_xl", [P, KC, P], f32r)
        gact = sb(st, name + "_g", [P, F])
        h = sb(st, name + "_h", [P, F])
        hh = sb(st, name + "_hh", [FP, KC, P], f32r)
        hl = sb(st, name + "_hl", [FP, KC, P], f32r)
        names = ("xhi", "xlo", "up", "silu", "h", "th", "hhi", "hlo", "dn")
        s = {n: sem(st, f"{name}_{n}") for n in names}
        XB, UB, GB, HB, YB = 0, 1, 2, 3, 4
        out_done = s["dn"]

        @block.tensor
        def _(pe):
            def turn_x(t, i, r):
                pe.wait_ge(s_ld[r], 16 * i + 16)
                for k in range(KC):
                    mm = nc.tensor.transpose(psum[:, XB, k * P:(k + 1) * P], xin[:, r, k * P:(k + 1) * P], ident[:, :])
                mm.then_inc(s_used, 1)

            def up(t):
                w = weights_of(pe, t, True)
                pe.wait_ge(s["xlo"], t + 1)
                for bank, col in ((UB, 0), (GB, W3)):
                    for k in range(KC):
                        for n, (a, part) in enumerate(((xh, 0), (xh, 1), (xl, 0))):
                            mm = nc.tensor.matmul(psum[:, bank, 0:F], a[:, k, :], w(P, part, col + k * F, F),
                                                  start=(k == 0 and n == 0), stop=(k == KC - 1 and n == 2))
                mm.then_inc(s["up"], 1)

            def turn_h(t):
                pe.wait_ge(s["h"], t + 1)
                for k in range(KC):
                    mm = nc.tensor.transpose(psum[0:FP, HB, k * P:(k + 1) * P], h[:, k * FP:(k + 1) * FP], ident[:, :])
                mm.then_inc(s["th"], 1)

            def down(t, w):
                pe.wait_ge(s["hlo"], t + 1)
                pe.wait_ge(s_y, t + 1)
                for k in range(KC):
                    for n, (a, part) in enumerate(((hh, 0), (hh, 1), (hl, 0))):
                        mm = nc.tensor.matmul(psum[:, YB, :], a[:, k, :], w(FP, part, W2 + k * HID, HID),
                                              start=(k == 0 and n == 0), stop=(k == KC - 1 and n == 2))
                mm.then_inc(s["dn"], 1)

            pe.sem_inc(s["dn"], 1)
            turn_x(0, 0, 0)
            up(0)
            turn_x(1, 0, 1)
            turn_h(0)
            with pe.Fori(0, n_tiles // 2 - 1) as i:
                for r in range(2):
                    t = 2 * i + 1 + r
                    up(t)
                    turn_x(t + 1, i + 1, r)
                    down(t - 1, weights_of(pe, t - 1, False))
                    turn_h(t)
            t = n_tiles - 1
            up(t)
            down(t - 1, weights_of(pe, t - 1, False))
            turn_h(t)
            down(t, weights_of(pe, t, False))

        @block.scalar
        def _(act):
            def silu(t):
                act.wait_ge(s["up"], t + 1)
                nc.scalar.activation(gact[:, :], psum[:, UB, 0:F], ACT.Silu, scale=score_of(t)).then_inc(s["silu"], 1)

            def split_x(t):
                act.wait_ge(s_used, t + 3)
                nc.scalar.activation(xh[:, :, :].rearrange("p c n -> p (c n)"), psum[:, XB, :], ACT.Copy
                                     ).then_inc(s["xhi"], 1)

            def split_h(t):
                act.wait_ge(s["th"], t + 1)
                nc.scalar.activation(hh[:, :, :].rearrange("p c n -> p (c n)"), psum[0:FP, HB, :], ACT.Copy
                                     ).then_inc(s["hhi"], 1)

            def store_ready(t, i, r):
                if shared:
                    return
                act.wait_ge(s["dn"], t + 2)
                act.wait_ge(s_st[r], 16 * i + 16)
                nc.scalar.activation(ybuf[:, r, :], psum[:, YB, :], ACT.Copy).then_inc(s_y, 1)

            split_x(0)
            silu(0)
            split_x(1)
            split_h(0)
            with act.Fori(0, n_tiles // 2 - 1) as i:
                for r in range(2):
                    t = 2 * i + 1 + r
                    silu(t)
                    split_x(t + 1)
                    store_ready(t - 1, i, r)
                    split_h(t)
            t = n_tiles - 1
            silu(t)
            store_ready(t - 1, n_tiles // 2 - 1, 0)
            split_h(t)
            store_ready(t, n_tiles // 2 - 1, 1)

        @block.vector
        def _(dve):
            def gated(t):
                dve.wait_ge(s["silu"], t + 1)
                nc.vector.scalar_tensor_tensor(out=h[:, :], in0=psum[:, GB, 0:F], scalar=score_of(t), in1=gact[:, :],
                                               op0=ALU.mult, op1=ALU.mult).then_inc(s["h"], 1)

            def rest_x(t):
                dve.wait_ge(s["xhi"], t + 1)
                nc.vector.tensor_tensor(xl[:, :, :].rearrange("p c n -> p (c n)"), psum[:, XB, :],
                                        xh[:, :, :].rearrange("p c n -> p (c n)").bitcast(f32), ALU.subtract
                                        ).then_inc(s["xlo"], 1)

            def rest_h(t):
                dve.wait_ge(s["hhi"], t + 1)
                nc.vector.tensor_tensor(hl[:, :, :].rearrange("p c n -> p (c n)"), psum[0:FP, HB, :],
                                        hh[:, :, :].rearrange("p c n -> p (c n)").bitcast(f32), ALU.subtract
                                        ).then_inc(s["hlo"], 1)

            def add_residual(t, i, r):
                if not shared:
                    return
                dve.wait_ge(s["dn"], t + 2)
                dve.wait_ge(residual[r], 16 * i + 16)
                nc.vector.tensor_tensor(ybuf[:, r, :], psum[:, YB, :], ybuf[:, r, :], ALU.add).then_inc(s_y, 1)

            rest_x(0)
            gated(0)
            rest_x(1)
            rest_h(0)
            with dve.Fori(0, n_tiles // 2 - 1) as i:
                for r in range(2):
                    t = 2 * i + 1 + r
                    gated(t)
                    rest_x(t + 1)
                    add_residual(t - 1, i, r)
                    rest_h(t)
            t = n_tiles - 1
            gated(t)
            add_residual(t - 1, n_tiles // 2 - 1, 0)
            rest_h(t)
            add_residual(t, n_tiles // 2 - 1, 1)

        return out_done

    def experts():
        NK = NT * TOPK
        with ExitStack() as outer:
            wbuf = sb(outer, "wbuf", [P, 2 * 2 * WW], f32r)
            table = sb(outer, "table", [1, 5, RT], i32)
            rlist = sb(outer, "rlist", [P, 2 * RT], i32)
            slot = sb(outer, "slot", [P, NK], i32)
            entry = sb(outer, "entry", [P, NK, 2], i32)
            s_wl = sem(outer, "s5_wl")

            def routing():
                with ExitStack() as st:
                    names3 = ("shifted", "expd", "score", "biased", "eq", "cand", "oh0", "oh1", "prod", "tot",
                              "incl", "posf")
                    a = {n: sb(st, "r_" + n, [P, NT, NE]) for n in names3}
                    row = {n: sb(st, "r_" + n, [P, NT, 1]) for n in ("mx", "sum", "inv", "best", "first", "p0", "p1",
                                                                     "tokf")}
                    ex = {n: sb(st, "r_" + n, [P, 1, NE]) for n in ("bias", "iota", "nt", "tsi", "ts",
                                                                    "base", "one8")}
                    tb = {n: sb(st, "r_" + n, [1, RT, NE]) for n in ("ge", "eqt")}
                    te = {n: sb(st, "r_" + n, [1, RT, 1]) for n in ("e", "flag", "iota_t")}
                    cnt_i = sb(st, "r_cnt_i", [P, 1, NE], i32)
                    lane_i = sb(st, "r_lane_i", [P, NT], i32)
                    tile_i = sb(st, "r_tile_i", [P, NT], i32)
                    half_i = sb(st, "r_half_i", [1, RT, 1], i32)
                    tri = sb(st, "r_tri", [P, P])
                    ones = sb(st, "r_ones", [P, P])
                    s_c, s_step, s_exp, s_m, s_cnt = (sem(st, "s4_c"), sem(st, "s4_step"), sem(st, "s4_exp"),
                                                      sem(st, "s4_m"), sem(st, "s4_cnt"))
                    s_in = sem(st, "s4_in")
                    block = st.enter_context(nc.Block())

                    @block.sync
                    def _(sp):
                        sp.dma_start(ex["bias"][:, 0, :], expert_bias).then_inc(s_in, 16)
                        sp.dma_start(ex["iota"][:, 0, :], c_expert).then_inc(s_in, 16)
                        sp.dma_start(row["tokf"][:, :, 0], c_token).then_inc(s_in, 16)
                        sp.dma_start(te["iota_t"][:, :, 0], c_tile).then_inc(s_in, 16)
                        sp.dma_start(tri[:, :], c_tri).then_inc(s_in, 16)

                    @block.scalar
                    def _(act):
                        act.wait_ge(s_exp, 1)
                        nc.scalar.activation(a["expd"][:, :, :], a["shifted"][:, :, :], ACT.Exp).then_inc(s_exp, 1)

                    @block.tensor
                    def _(pe):
                        pe.wait_ge(s_m, 1)
                        flat = a["prod"][:, :, :].rearrange("p t e -> p (t e)")
                        nc.tensor.matmul(psum[:, 0, 0:NT * NE], tri[:, :], flat, start=True, stop=True)
                        nc.tensor.matmul(psum[:, 1, 0:NT * NE], ones[:, :], flat, start=True, stop=True
                                         ).then_inc(s_cnt, 1)

                    @block.vector
                    def _(dve):
                        steps_done = [0]

                        def then(ins):
                            steps_done[0] += 1
                            ins.then_inc(s_step, 1)
                            dve.wait_ge(s_step, steps_done[0])

                        v = nc.vector
                        TE = [P, NT, NE]
                        then(v.memset(ones[:, :], 1.0))
                        then(v.memset(ex["one8"][:, :, :], 1.0))
                        then(v.reduce_max(row["mx"][:, :, 0], logits[:, :, :], axis=AX.X))
                        then(v.tensor_tensor(a["shifted"][:, :, :], logits[:, :, :],
                                             row["mx"][:, :, :].to_broadcast(TE), ALU.subtract))
                        dve.sem_inc(s_exp, 1)
                        dve.wait_ge(s_exp, 2)
                        then(v.reduce_sum(row["sum"][:, :, 0], a["expd"][:, :, :], axis=AX.X))
                        then(v.reciprocal(row["inv"][:, :, :], row["sum"][:, :, :]))
                        then(v.tensor_tensor(a["score"][:, :, :], a["expd"][:, :, :],
                                             row["inv"][:, :, :].to_broadcast(TE), ALU.mult))
                        dve.wait_ge(s_in, 80)
                        then(v.tensor_tensor(a["biased"][:, :, :], a["score"][:, :, :],
                                             ex["bias"][:, :, :].to_broadcast(TE), ALU.add))
                        entries = entry[:, :, :].rearrange("p (t k) e -> p t k e", k=TOPK)
                        for k, oh in enumerate(("oh0", "oh1")):
                            then(v.reduce_max(row["best"][:, :, 0], a["biased"][:, :, :], axis=AX.X))
                            then(v.tensor_tensor(a["eq"][:, :, :], a["biased"][:, :, :],
                                                 row["best"][:, :, :].to_broadcast(TE), ALU.is_equal))
                            then(v.scalar_tensor_tensor(out=a["cand"][:, :, :], in0=a["eq"][:, :, :],
                                                        scalar=-float(NE), in1=ex["iota"][:, :, :].to_broadcast(TE),
                                                        op0=ALU.mult, op1=ALU.add))
                            then(v.tensor_reduce(row["first"][:, :, 0], a["cand"][:, :, :], axis=AX.X, op=ALU.min))
                            then(v.tensor_tensor(a[oh][:, :, :], a["cand"][:, :, :],
                                                 row["first"][:, :, :].to_broadcast(TE), ALU.is_equal))
                            then(v.scalar_tensor_tensor(out=a["biased"][:, :, :], in0=a[oh][:, :, :], scalar=MASKED,
                                                        in1=a["biased"][:, :, :], op0=ALU.mult, op1=ALU.add))
                            then(v.tensor_tensor(a["eq"][:, :, :], a[oh][:, :, :], a["score"][:, :, :], ALU.mult))
                            then(v.reduce_sum(entries[:, :, k, 1].bitcast(f32), a["eq"][:, :, :], axis=AX.X))
                            then(v.tensor_copy(entries[:, :, k, 0], row["tokf"][:, :, 0]))
                        then(v.tensor_tensor(a["prod"][:, :, :], a["oh0"][:, :, :], a["oh1"][:, :, :], ALU.add))
                        dve.sem_inc(s_m, 1)
                        dve.wait_ge(s_cnt, 1)
                        then(v.tensor_copy(a["tot"][:, :, :],
                                           psum[:, 1, 0:NT * NE].rearrange("p (t e) -> p t e", e=NE)))
                        for e in range(NE):
                            then(v.tensor_tensor_scan(a["incl"][:, :, e], ones[:, 0:NT], a["tot"][:, :, e], 0.0,
                                                      ALU.mult, ALU.add))
                        cnt = a["incl"][:, NT - 1:NT, :]
                        then(v.tensor_scalar(cnt_i[:, :, :], cnt, float(P - 1), None, ALU.add))
                        then(v.tensor_scalar(cnt_i[:, :, :], cnt_i[:, :, :], PLOG, None, ALU.logical_shift_right))
                        then(v.tensor_scalar(ex["nt"][:, :, :], cnt_i[:, :, :], 1.0, None, ALU.max))
                        then(v.tensor_tensor_scan(ex["tsi"][:, 0, :], ex["one8"][:, 0, :], ex["nt"][:, 0, :], 0.0,
                                                  ALU.mult, ALU.add))
                        then(v.tensor_tensor(ex["ts"][:, :, :], ex["tsi"][:, :, :], ex["nt"][:, :, :], ALU.subtract))
                        then(v.tensor_scalar(ex["base"][:, :, :], ex["ts"][:, :, :], float(P), None, ALU.mult))
                        then(v.tensor_tensor(a["posf"][:, :, :], a["incl"][:, :, :], a["tot"][:, :, :], ALU.subtract))
                        then(v.tensor_tensor(a["posf"][:, :, :], a["posf"][:, :, :],
                                             ex["base"][:, :, :].to_broadcast(TE), ALU.add))
                        then(v.tensor_tensor(a["posf"][:, :, :],
                                             psum[:, 0, 0:NT * NE].rearrange("p (t e) -> p t e", e=NE),
                                             a["posf"][:, :, :], ALU.add))
                        slots = slot[:, :].rearrange("p (t k) -> p t k", k=TOPK)
                        for k, oh in enumerate(("oh0", "oh1")):
                            p = row[f"p{k}"]
                            then(v.tensor_tensor(a["eq"][:, :, :], a[oh][:, :, :], a["posf"][:, :, :], ALU.mult))
                            then(v.reduce_sum(p[:, :, 0], a["eq"][:, :, :], axis=AX.X))
                            then(v.tensor_copy(pos[:, k, :], p[:, :, 0]))
                            then(v.tensor_scalar(lane_i[:, :], pos[:, k, :], P - 1, None, ALU.bitwise_and))
                            then(v.tensor_scalar(tile_i[:, :], pos[:, k, :], PLOG, None, ALU.logical_shift_right))
                            then(v.scalar_tensor_tensor(out=slots[:, :, k], in0=lane_i[:, :],
                                                        scalar=float(RT), in1=tile_i[:, :],
                                                        op0=ALU.mult, op1=ALU.add))
                        R = [1, RT, NE]
                        it = te["iota_t"][:, :, :].to_broadcast(R)
                        then(v.tensor_tensor(tb["ge"][:, :, :], it, ex["tsi"][0:1, :, :].to_broadcast(R), ALU.is_ge))
                        then(v.reduce_sum(te["e"][:, :, 0], tb["ge"][:, :, :], axis=AX.X))
                        then(v.tensor_scalar(te["e"][:, :, :], te["e"][:, :, :], float(NE - 1), None, ALU.min))
                        then(v.tensor_tensor(tb["eqt"][:, :, :], it, ex["ts"][0:1, :, :].to_broadcast(R), ALU.is_equal))
                        then(v.reduce_sum(te["flag"][:, :, 0], tb["eqt"][:, :, 0:NE - 1], axis=AX.X))
                        then(v.tensor_scalar(half_i[:, :, :], te["e"][:, :, :], 1.0, None, ALU.add))
                        then(v.tensor_scalar(half_i[:, :, :], half_i[:, :, :], 1, None, ALU.bitwise_and))
                        then(v.tensor_scalar(table[:, 0, :], half_i[:, :, 0], 2.0 * WW, None, ALU.mult))
                        then(v.tensor_scalar(table[:, 1, :], te["e"][:, :, 0], 32.0, 64.0, ALU.mult, ALU.add))
                        then(v.tensor_copy(table[:, 2, :], te["flag"][:, :, 0]))
                        then(v.tensor_scalar(table[:, 3, :], te["e"][:, :, 0], float(WW), 2.0 * WW, ALU.mult, ALU.add))
                        then(v.tensor_scalar(table[:, 4, :], half_i[:, :, 0], -2.0 * WW, 2.0 * WW,
                                             ALU.mult, ALU.add))

            def shared_expert():
                with ExitStack() as st:
                    xin = sb(st, "xin5", [P, 2, HID])
                    ybuf = sb(st, "y5", [P, 2, HID])
                    idx = sb(st, "idx5", [P, 16], i32)
                    ent = sb(st, "ent5", [P, 32], i32)
                    s_ld = [sem(st, f"s5_ld{r}") for r in range(2)]
                    s_used, s_y = sem(st, "s5_used"), sem(st, "s5_y")
                    s_st = [sem(st, f"s5_st{r}") for r in range(2)]
                    s_fill = [sem(st, f"s5_fill{r}") for r in range(2)]
                    s_cp, s_sc, s_rl = sem(st, "s5_cp"), sem(st, "s5_sc"), sem(st, "s5_rl")
                    block = st.enter_context(nc.Block())

                    def weights_of(pe, t, first_use):
                        return lambda rows, part, col, width: wbuf[0:rows, part * WW + col:part * WW + col + width]

                    @block.sync
                    def _(sp):
                        for e in range(2):
                            for part in range(2):
                                sp.dma_start(wbuf[:, (2 * e + part) * WW:(2 * e + part + 1) * WW].bitcast(f32),
                                             w_dram[part, :, e * WW:(e + 1) * WW]).then_inc(s_wl, 16)
                            if e == 0:
                                sp.wait_ge(s_wl, 32)

                        def load(t, r):
                            sp.wait_ge(s_used, t + 1)
                            sp.dma_start(xin[:, r, :], x1_dram[ds(t * P, P), :]).then_inc(s_ld[r], 16)

                        def fill(t, i, r):
                            sp.wait_ge(s_st[r], 16 * i + 16)
                            sp.dma_start(ybuf[:, r, :], x1_dram[ds(t * P, P), :]).then_inc(s_fill[r], 16)

                        def store(t, r):
                            sp.wait_ge(s_y, t + 2)
                            sp.dma_start(y_dram[ds(t * P, P), :], ybuf[:, r, :]).then_inc(s_st[r], 16)

                        sp.sem_inc(s_st[0], 16)
                        sp.sem_inc(s_st[1], 16)
                        for r in range(2):
                            load(r, r)
                            fill(r, 0, r)
                        with sp.Fori(0, NT // 2 - 1) as i:
                            for r in range(2):
                                t = 2 * i + r
                                load(t + 2, r)
                                store(t, r)
                                fill(t + 2, i + 1, r)
                        store(NT - 2, 0)
                        store(NT - 1, 1)
                        for r in range(2):
                            sp.wait_ge(s_st[r], 16 + 16 * (NT // 2))
                        sp.wait_ge(s_wl, 64)

                    @block.gpsimd
                    def _(pool):
                        with pool.Fori(0, NK // 16) as m:
                            pool.tensor_copy(idx[:, :], slot[:, ds(16 * m, 16)]).then_inc(s_cp, 1)
                            pool.tensor_copy(ent[:, :], entry[:, :, :].rearrange("p n e -> p (n e)")[:, ds(32 * m, 32)]
                                             ).then_inc(s_cp, 1)
                            wait_alone(pool, s_cp, 2 * m + 2)
                            for n in range(16):
                                pool.indirect_dma_start(
                                    list_dram, bass.IndirectOffsetOnAxis(ap=idx[:, n:n + 1], axis=0),
                                    ent[:, 2 * n:2 * n + 2], None).then_inc(s_sc, 16)
                            wait_alone(pool, s_sc, 256 * m + 256)
                        pool.dma_start(rlist[:, :], list_dram.rearrange("(p t) e -> p (t e)", p=P)).then_inc(s_rl, 16)
                        wait_alone(pool, s_rl, 16)

                    @block.scalar
                    def _(act):
                        act.sem_inc(s_used, 2)
                        act.sem_inc(s_y, 1)

                    @block.tensor
                    def _(pe):
                        pe.wait_ge(s_wl, 32)

                    expert_tiles(st, "e5", NT, True, block, xin, ybuf, lambda t: 1.0, weights_of,
                                 s_ld, s_used, s_y, s_st, residual=s_fill)

            def routed_experts():
                with ExitStack() as st:
                    xin = sb(st, "xin6", [P, 2, HID])
                    ybuf = sb(st, "y6", [P, 2, HID])
                    idx = sb(st, "idx6", [P, 2], i32)
                    s_ld = [sem(st, f"s6_ld{r}") for r in range(2)]
                    s_used, s_y, s_cp = sem(st, "s6_used"), sem(st, "s6_y"), sem(st, "s6_cp")
                    s_st = [sem(st, f"s6_st{r}") for r in range(2)]
                    block = st.enter_context(nc.Block())

                    def weights_of(pe, t, first_use):
                        if first_use:
                            need = pe.value_load(table[0:1, 1, ds(t, 1)], min_val=64, max_val=32 * (NE + 1))
                            wait_alone(pe, s_wl, need)
                        base = pe.value_load(table[0:1, 0, ds(t, 1)], min_val=0, max_val=2 * WW)
                        return lambda rows, part, col, width: wbuf[0:rows, ds(base + part * WW + col, width)]

                    @block.scalar
                    def _(act):
                        act.sem_inc(s_used, 2)
                        act.sem_inc(s_y, 1)

                    done = expert_tiles(st, "e6", RT, False, block, xin, ybuf,
                                        lambda t: rlist[:, ds(2 * t + 1, 1)].bitcast(f32), weights_of,
                                        s_ld, s_used, s_y, s_st)

                    @block.gpsimd
                    def _(pool):
                        with pool.Fori(0, RT // 2) as i:
                            for r in range(2):
                                t = 2 * i + r
                                wait_alone(pool, s_used, t + 1)
                                pool.tensor_copy(idx[:, r:r + 1], rlist[:, ds(2 * t, 1)]).then_inc(s_cp, 1)
                                wait_alone(pool, s_cp, t + 1)
                                pool.indirect_dma_start(xin[:, r, :], None, x1_dram,
                                                        bass.IndirectOffsetOnAxis(ap=idx[:, r:r + 1], axis=0)
                                                        ).then_inc(s_ld[r], 16)

                    @block.sync
                    def _(sp):
                        sp.sem_inc(s_st[0], 16)
                        sp.sem_inc(s_st[1], 16)

                        def next_weights(t):
                            flag = sp.value_load(table[0:1, 2, ds(t, 1)], min_val=0, max_val=1)
                            with sp.If(flag > 0):
                                need = sp.value_load(table[0:1, 1, ds(t, 1)], min_val=64, max_val=32 * (NE + 1))
                                src = sp.value_load(table[0:1, 3, ds(t, 1)], min_val=0, max_val=NE * WW)
                                dst = sp.value_load(table[0:1, 4, ds(t, 1)], min_val=0, max_val=2 * WW)
                                wait_alone(sp, s_wl, need)
                                wait_alone(sp, done, t + 1)
                                for part in range(2):
                                    sp.dma_start(wbuf[:, ds(dst + part * WW, WW)].bitcast(f32),
                                                 w_dram[part, :, ds(src, WW)]).then_inc(s_wl, 16)

                        def store(t, r):
                            sp.wait_ge(s_y, t + 2)
                            sp.dma_start(r_dram[ds(t * P, P), :], ybuf[:, r, :]).then_inc(s_st[r], 16)

                        next_weights(0)
                        with sp.Fori(0, RT // 2 - 1) as i:
                            for r in range(2):
                                t = 2 * i + r
                                next_weights(t + 1)
                                store(t, r)
                        next_weights(RT - 1)
                        store(RT - 2, 0)
                        store(RT - 1, 1)
                        for r in range(2):
                            sp.wait_ge(s_st[r], 16 + 16 * (RT // 2))

            routing()
            shared_expert()
            routed_experts()

    def combine():
        with ExitStack() as st:
            ys = sb(st, "ys7", [P, 2, HID])
            g0 = sb(st, "g07", [P, 2, HID])
            g1 = sb(st, "g17", [P, 2, HID])
            o = sb(st, "o7", [P, 2, HID])
            idx = sb(st, "idx7", [P, 2, TOPK], i32)
            stats = sb(st, "stats7", [P, 6])
            mv = sb(st, "mv7", [P, 2])
            std = sb(st, "std7", [P, 1])
            rstd = sb(st, "rstd7", [P, 1])
            s_ld = [sem(st, f"s7_ld{r}") for r in range(2)]
            s_gt = [sem(st, f"s7_gt{r}") for r in range(2)]
            s_st = [sem(st, f"s7_st{r}") for r in range(2)]
            s_cp, s_ln, s_o = sem(st, "s7_cp"), sem(st, "s7_ln"), sem(st, "s7_o")
            s_var, s_std = sem(st, "s7_var"), sem(st, "s7_std")
            block = st.enter_context(nc.Block())

            @block.sync
            def _(sp):
                with sp.Fori(0, NT // 2) as i:
                    for r in range(2):
                        t = 2 * i + r
                        sp.wait_ge(s_o, t + 1)
                        sp.dma_start(ys[:, r, :], y_dram[ds(t * P, P), :]).then_inc(s_ld[r], 16)

            @block.scalar
            def _(act):
                act.sem_inc(s_st[0], 16)
                act.sem_inc(s_st[1], 16)
                act.sem_inc(s_o, 2)
                with act.Fori(0, NT // 2) as i:
                    for r in range(2):
                        t = 2 * i + r
                        act.wait_ge(s_var, t + 1)
                        nc.scalar.activation(std[:, :], mv[:, 1:2], ACT.Sqrt).then_inc(s_std, 1)
                        act.wait_ge(s_o, t + 3)
                        act.dma_start(out[ds(t * P, P), :], o[:, r, :]).then_inc(s_st[r], 16)
                for r in range(2):
                    act.wait_ge(s_st[r], 16 + 16 * (NT // 2))

            @block.gpsimd
            def _(pool):
                with pool.Fori(0, NT // 2) as i:
                    for r in range(2):
                        t = 2 * i + r
                        wait_alone(pool, s_o, t + 1)
                        for k in range(TOPK):
                            pool.tensor_copy(idx[:, r, k:k + 1], pos[:, k, ds(t, 1)]).then_inc(s_cp, 1)
                        wait_alone(pool, s_cp, TOPK * t + TOPK)
                        for k, g in enumerate((g0, g1)):
                            pool.indirect_dma_start(g[:, r, :], None, r_dram,
                                                    bass.IndirectOffsetOnAxis(ap=idx[:, r, k:k + 1], axis=0)
                                                    ).then_inc(s_gt[r], 16)

            @block.vector
            def _(dve):
                v = nc.vector
                LN = 5
                with dve.Fori(0, NT // 2) as i:
                    for r in range(2):
                        t = 2 * i + r
                        dve.wait_ge(s_ld[r], 16 * i + 16)
                        dve.wait_ge(s_gt[r], 32 * i + 32)
                        v.tensor_tensor(g0[:, r, :], g0[:, r, :], g1[:, r, :], ALU.add).then_inc(s_ln, 1)
                        dve.wait_ge(s_ln, LN * t + 1)
                        v.tensor_tensor(ys[:, r, :], ys[:, r, :], g0[:, r, :], ALU.add).then_inc(s_ln, 1)
                        dve.wait_ge(s_ln, LN * t + 2)
                        v.bn_stats(stats[:, :], ys[:, r, :]).then_inc(s_ln, 1)
                        wait_alone(dve, s_ln, LN * t + 3)
                        v.bn_aggr(mv[:, :], stats[:, :]).then_inc(s_ln, 1)
                        dve.wait_ge(s_ln, LN * t + 4)
                        v.tensor_scalar(mv[:, 1:2], mv[:, 1:2], EPS, None, ALU.add).then_inc(s_var, 1)
                        dve.wait_ge(s_std, t + 1)
                        v.reciprocal(rstd[:, :], std[:, :]).then_inc(s_ln, 1)
                        dve.wait_ge(s_ln, LN * t + 5)
                        dve.wait_ge(s_st[r], 16 * i + 16)
                        v.tensor_scalar(o[:, r, :], ys[:, r, :], mv[:, 0:1], rstd[:, :],
                                        ALU.subtract, ALU.mult).then_inc(s_o, 1)

    with top:
        projections()
        attention()
        post_attention()
        experts()
        combine()


def kernel(**inputs):
    import numpy as np
    import concourse.bacc as bacc
    from concourse import mybir
    from concourse.bass_utils import run_bass_kernel_spmd

    a = {n.replace("L0_", ""): np.asarray(v) for n, v in inputs.items()}
    x = a["attn_hidden_states"]
    B, T, HID = x.shape
    D = a["attn_Wk"].shape[0]
    H = HID // D
    NE, _, F = a["ffn_w1"].shape
    TOPK, P = 2, 128
    N = B * T
    NT, KC = N // P, HID // P
    RT = TOPK * NT + NE
    FP = F // KC

    order = np.concatenate([np.arange(0, D, 2), np.arange(1, D, 2)])
    heads = (np.arange(H)[:, None] * D + order[None, :]).reshape(-1)
    half = D // 2
    theta = (1.0 / 10000.0 ** (np.arange(0, half, 2, dtype=np.float32) / half)).astype(np.float32)
    angle = (np.arange(H, dtype=np.float32)[:, None] * np.tile(theta, 2)[None, :]).astype(np.float32)
    cos = np.ascontiguousarray(np.broadcast_to(np.cos(angle), (P, H, half)), dtype=np.float32)
    sin = np.ascontiguousarray(np.broadcast_to(np.sin(angle), (P, H, half)), dtype=np.float32)

    def expert(w1, w3, w2):
        up = [w.reshape(KC, P, F).transpose(1, 0, 2).reshape(P, KC * F) for w in (w1, w3)]
        down = np.zeros((P, KC, HID), np.float32)
        down[:FP] = w2.reshape(KC, FP, HID).transpose(1, 0, 2)
        return np.concatenate(up + [down.reshape(P, KC * HID)], axis=1)

    w_all = np.concatenate([expert(a["ffn_sw1"], a["ffn_sw3"], a["ffn_sw2"])] +
                           [expert(a["ffn_w1"][e], a["ffn_w3"][e], a["ffn_w2"][e]) for e in range(NE)], axis=1)
    wk_t = a["attn_Wk"][order].T
    arrays = {
        "x": x.reshape(N, HID),
        "x_t": x.reshape(N, HID).T,
        "wq_t": a["attn_Wq"][heads].T,
        "wk_t": np.concatenate([wk_t, wk_t, wk_t], axis=1),
        "wv_t": a["attn_Wv"].T,
        "wo_t": a["attn_Wo"].T,
        "rope_cos": cos,
        "rope_sin": sin,
        "gate_w": a["ffn_gate_w"],
        "expert_bias": np.broadcast_to(a["ffn_expert_bias"], (P, NE)),
        "w_all": w_all,
        "c_expert": np.broadcast_to(np.arange(NE, dtype=np.float32), (P, NE)),
        "c_token": np.arange(P, dtype=np.float32)[:, None] + P * np.arange(NT, dtype=np.float32)[None, :],
        "c_tile": np.arange(RT, dtype=np.float32)[None, :],
        "c_tri": np.triu(np.ones((P, P), np.float32), 1),
    }
    nc = bacc.Bacc("TRN2", target_bir_lowering=False, num_devices=1)
    arrays = {n: np.ascontiguousarray(v) for n, v in arrays.items()}
    args = {n: nc.dram_tensor("in_" + n, v.shape, mybir.dt.from_np(v.dtype), kind="ExternalInput").ap()
            for n, v in arrays.items()}
    out = nc.dram_tensor("out_0_dram", (N, HID), mybir.dt.float32, kind="ExternalOutput").ap()
    build(nc, B, T, HID, H, F, NE, TOPK, out=out, **args)
    r = run_bass_kernel_spmd(nc, [{"in_" + n: v for n, v in arrays.items()}], core_ids=[0])
    return r.results[0]["out_0_dram"].reshape(B, T, HID)
```

```python
import concourse.bass as bass
from concourse import mybir
from contextlib import ExitStack


def build(nc, B, T, HID, H, F, NE, TOPK,
          x, x_t, wq_t, wkv_t, wo_t, rope_cos, rope_sin, gate_w, expert_bias, w_all,
          c_expert, c_token, c_tile, c_tri, out):
    f32, f32r, bf16, i32 = mybir.dt.float32, mybir.dt.float32r, mybir.dt.bfloat16, mybir.dt.int32
    ALU, ACT, AX = mybir.AluOpType, mybir.ActivationFunctionType, mybir.AxisListType
    ds = bass.ds

    P, PLOG = 128, 7
    N = B * T
    D = HID // H
    KC = HID // P
    HG = P // D
    NG = H // HG
    CH = 512
    NCH = N // CH
    QT = T // P
    NU = B * NG
    NT = N // P
    RT = TOPK * NT + NE
    FP = F // KC
    W3, W2, WW = KC * F, 2 * KC * F, 2 * KC * F + KC * HID
    SCALE = float(D) ** -0.5
    MASKED = -1e30
    EPS = 1e-5
    SPLIT = 1584
    NSPLIT = (NE + 1) * WW // SPLIT
    VW = 2 * D + 1
    SR = 3 * D
    assert NSPLIT * SPLIT == (NE + 1) * WW

    def dram(name, shape, dt):
        return nc.dram_tensor(name, shape, dt).ap()

    q_dram = dram("q_dram", (2, NG, HG, D, N), f32)
    k_dram = dram("k_dram", (SR + 1, N), f32)
    v_dram = dram("v_dram", (P, NT, VW), f32)
    w_dram = dram("w_dram", (2, P, (NE + 1) * WW), f32)
    attn_dram = dram("attn_dram", (N, HID), f32)
    x1_dram = dram("x1_dram", (N, HID), f32)
    y_dram = dram("y_dram", (N, HID), f32)
    r_dram = dram("r_dram", (RT * P, HID), f32)
    list_dram = dram("list_dram", (P * RT, 2), i32)

    top = ExitStack()

    def sem(stack, name):
        return stack.enter_context(nc.semaphore(name))

    def sb(stack, name, shape, dt=f32):
        return stack.enter_context(nc.sbuf_tensor(name, shape, dt))

    def wait_alone(eng, s, value):
        eng.wait_ge(s, value)
        eng.sem_inc(s_passed, 1)

    s_passed = sem(top, "s_passed")
    psum = top.enter_context(nc.psum_tensor("psum", [P, 8, 512], f32))
    ident = sb(top, "ident", [P, P])
    identb = sb(top, "identb", [P, P], bf16)
    mask_q = sb(top, "mask_q", [P, P], bf16)
    mask_k = sb(top, "mask_k", [P, HG, P], bf16)
    logits = sb(top, "logits", [P, NT, NE])
    pos = sb(top, "pos", [P, TOPK, NT], i32)

    def projections():
        with ExitStack() as st:
            xt = sb(st, "xt", [P, 2, KC, CH])
            xh = sb(st, "xh", [P, 2, KC, CH], f32r)
            xl = sb(st, "xl", [P, 2, KC, CH], f32r)
            w = sb(st, "w", [P, KC, P + HID])
            wh = sb(st, "wh", [P, KC, P + HID], f32r)
            wl = sb(st, "wl", [P, KC, P + HID], f32r)
            wq = sb(st, "wq", [P, KC, H, 2, D // 2])
            cos = sb(st, "cos", [P, H, D // 2])
            sin = sb(st, "sin", [P, H, D // 2])
            t1 = sb(st, "t1", [P, 2, H, D // 2])
            kst = sb(st, "kst", [SR + 1, 2, CH], f32r)
            vt = sb(st, "vt", [P, CH])
            vst = sb(st, "vst", [P, 2, CH // P, VW], f32r)
            qhi = sb(st, "qhi", [P, 2, CH], f32r)
            qlo = sb(st, "qlo", [P, 2, CH], f32r)
            s_w, s_wkv, s_rot, s_step = sem(st, "s1_w"), sem(st, "s1_wkv"), sem(st, "s1_rot"), sem(st, "s1_step")
            s_x = [sem(st, f"s1_x{r}") for r in range(2)]
            s_xh, s_xl, s_mm, s_ev = sem(st, "s1_xh"), sem(st, "s1_xl"), sem(st, "s1_mm"), sem(st, "s1_ev")
            s_hi, s_init, s_k, s_vt, s_vh = (sem(st, "s1_hi"), sem(st, "s1_init"), sem(st, "s1_k"), sem(st, "s1_vt"),
                                             sem(st, "s1_vh"))
            s_kv = [sem(st, f"s1_kv{r}") for r in range(2)]
            s_q = [sem(st, f"s1_q{r}") for r in range(2)]
            s_list = sem(st, "s1_list")
            zero = sb(st, "zero", [P, 2 * RT], i32)
            UN = 2 + NG
            MM0 = 2 * UN
            block = st.enter_context(nc.Block())

            @block.sync
            def _(sp):
                sp.dma_start(wq[:, :, :, :, :].rearrange("p c h e d -> p c (h e d)"),
                             wq_t.rearrange("(c p) n -> p c n", p=P)).then_inc(s_w, 16)
                sp.dma_start(cos[:, :, :], rope_cos).then_inc(s_w, 16)
                sp.dma_start(sin[:, :, :], rope_sin).then_inc(s_w, 16)
                sp.dma_start(w[:, :, 0:P], wkv_t.rearrange("(c p) n -> p c n", p=P)).then_inc(s_wkv, 16)
                for r in range(2):
                    sp.sem_inc(s_kv[r], 32)
                    sp.sem_inc(s_q[r], 32)
                with sp.Fori(0, NCH // 2) as i:
                    for r in range(2):
                        c = 2 * i + r
                        for g in range(NG):
                            sp.wait_ge(s_ev, UN * c + UN + 2 + g)
                            for part, src in ((0, qhi), (1, qlo)):
                                dst = q_dram[part, g].rearrange("j d n -> (j d) n")
                                sp.dma_start(dst[:, ds(c * CH, CH)], src[:, g % 2, :].bitcast(f32)
                                             ).then_inc(s_q[g % 2], 16)
                        sp.wait_ge(s_ev, UN * c + UN + UN)
                        sp.dma_start(k_dram[:, ds(c * CH, CH)], kst[:, r, :].bitcast(f32)).then_inc(s_kv[r], 16)
                        sp.dma_start(v_dram[:, ds(c * (CH // P), CH // P), :],
                                     vst[:, r, :, :].bitcast(f32)).then_inc(s_kv[r], 16)
                for r in range(2):
                    sp.wait_ge(s_kv[r], 32 + 32 * (NCH // 2))
                    sp.wait_ge(s_q[r], 32 + 32 * NCH * (NG // 2))

            @block.gpsimd
            def _(pool):
                x_cols = x_t.rearrange("(c p) n -> p c n", p=P)

                def load(c, r):
                    wait_alone(pool, s_xl, c + 1)
                    pool.dma_start(xt[:, r, :, :], x_cols[:, :, ds(c * CH, CH)]).then_inc(s_x[r], 16)

                load(0, 0)
                load(1, 1)
                pool.memset(ident[:, :], 0.0).then_inc(s_init, 1)
                pool.memset(mask_q[:, :], 0.0).then_inc(s_init, 1)
                pool.memset(mask_k[:, :, :], 0.0).then_inc(s_init, 1)
                pool.memset(zero[:, :], 0).then_inc(s_init, 1)
                pool.wait_ge(s_init, 4)
                pool.affine_select(out=ident[:, :], in_=ident[:, :], compare_op=ALU.not_equal, fill=1.0,
                                   base=0, pattern=[[-1, P]], channel_multiplier=1).then_inc(s_init, 1)
                pool.affine_select(out=mask_q[:, :], in_=mask_q[:, :], compare_op=ALU.is_ge, fill=MASKED,
                                   base=0, pattern=[[-1, P]], channel_multiplier=1).then_inc(s_init, 1)
                pool.affine_select(out=mask_k[:, :, :], in_=mask_k[:, :, :], compare_op=ALU.is_ge, fill=MASKED,
                                   base=0, pattern=[[0, HG], [1, P]], channel_multiplier=-1).then_inc(s_init, 1)
                pool.wait_ge(s_init, 7)
                pool.tensor_copy(identb[:, :], ident[:, :]).then_inc(s_init, 1)
                pool.dma_start(list_dram.rearrange("(p t) e -> p (t e)", p=P), zero[:, :]).then_inc(s_list, 16)
                with pool.Fori(1, NCH // 2) as i:
                    for r in range(2):
                        load(2 * i + r, r)
                pool.wait_ge(s_list, 16)

            @block.tensor
            def _(pe):
                pe.wait_ge(s_rot, 1)
                pe.wait_ge(s_init, 8)
                with pe.Fori(0, NCH // 2) as i:
                    for r in range(2):
                        c = 2 * i + r
                        pe.wait_ge(s_xl, c + 3)
                        for n in range(1 + NG):
                            pe.wait_ge(s_ev, UN * c + n + 1)
                            for k in range(KC):
                                for m, (a, b) in enumerate(((wh, xh), (wl, xh), (wh, xl))):
                                    mm = nc.tensor.matmul(psum[:, n, :], a[:, k, n * P:(n + 1) * P], b[:, r, k, :],
                                                          start=(k == 0 and m == 0), stop=(k == KC - 1 and m == 2))
                            mm.then_inc(s_mm, 1)
                        wait_alone(pe, s_vt, c + 1)
                        wait_alone(pe, s_ev, UN * c + UN)
                        for j in range(CH // P):
                            mm = nc.tensor.transpose(psum[:, NG + 1, j * D:(j + 1) * D],
                                                     vt[SR:P, j * P:(j + 1) * P], ident[SR:P, SR:P])
                        mm.then_inc(s_mm, 1)

            def chunks(eng, body):
                with eng.Fori(0, NCH // 2 - 1) as i:
                    for r in range(2):
                        body(2 * i + r, i, r, True)
                for r in range(2):
                    body(NCH - 2 + r, NCH // 2 - 1, r, r == 0)

            @block.vector
            def _(dve):
                dve.sem_inc(s_ev, UN)
                dve.sem_inc(s_xl, 2)
                dve.wait_ge(s_w, 48)
                turned = w[:, :, P:].rearrange("p c (h e d) -> p c h e d", e=2, d=D // 2)
                for k in range(KC):
                    a, b = wq[:, k, :, 0, :], wq[:, k, :, 1, :]
                    for half, (first, second, op) in enumerate(((cos, sin, ALU.subtract), (sin, cos, ALU.add))):
                        n = 2 * k + half
                        if n >= 1:
                            dve.wait_ge(s_step, 3 * n)
                        nc.vector.tensor_tensor(t1[:, 0], a, first[:, :, :], ALU.mult).then_inc(s_step, 1)
                        nc.vector.tensor_tensor(t1[:, 1], b, second[:, :, :], ALU.mult).then_inc(s_step, 1)
                        dve.wait_ge(s_step, 3 * n + 2)
                        nc.vector.tensor_tensor(turned[:, k, :, half, :], t1[:, 0], t1[:, 1], op).then_inc(s_step, 1)
                dve.wait_ge(s_step, 6 * KC)
                dve.wait_ge(s_wkv, 16)
                nc.vector.tensor_copy(wh[:, :, :], w[:, :, :]).then_inc(s_step, 1)
                dve.wait_ge(s_step, 6 * KC + 1)
                nc.vector.tensor_tensor(wl[:, :, :], w[:, :, :], wh[:, :, :].bitcast(f32), ALU.subtract
                                        ).then_inc(s_rot, 1)
                nc.vector.memset(kst[SR:SR + 1, :, :].bitcast(f32), 1.0).then_inc(s_k, 1)
                nc.vector.memset(vst[:, :, :, D:D + 1].bitcast(f32), 1.0).then_inc(s_k, 1)
                dve.wait_ge(s_k, 2)

                def rest_of_x(c, r):
                    dve.wait_ge(s_xh, c + 1)
                    nc.vector.tensor_tensor(xl[:, r, :, :], xt[:, r, :, :], xh[:, r, :, :].bitcast(f32), ALU.subtract
                                            ).then_inc(s_xl, 1)

                def chunk(c, i, r, prepare):
                    dve.wait_ge(s_kv[r], 32 * i + 32)
                    dve.wait_ge(s_mm, UN * c + MM0 + 1)
                    nc.vector.tensor_copy(kst[0:SR, r, :], psum[0:SR, 0, :]).then_inc(s_k, 1)
                    nc.vector.tensor_copy(vt[SR:P, :], psum[SR:P, 0, :]).then_inc(s_vt, 1)
                    dve.wait_ge(s_k, c + 3)
                    nc.vector.tensor_tensor(kst[2 * D:SR, r, :], psum[2 * D:SR, 0, :],
                                            kst[2 * D:SR, r, :].bitcast(f32), ALU.subtract).then_inc(s_ev, 1)
                    for g in range(NG):
                        dve.wait_ge(s_hi, NG * c + g + 1)
                        nc.vector.tensor_tensor(qlo[:, g % 2, :], psum[:, 1 + g, :],
                                                qhi[:, g % 2, :].bitcast(f32), ALU.subtract).then_inc(s_ev, 1)
                        if g == NG // 2 and prepare:
                            rest_of_x(c + 1, 1 - r)
                    dve.wait_ge(s_mm, UN * c + MM0 + UN)
                    v_turned = psum[:, NG + 1, 0:CH // P * D].rearrange("p (j d) -> p j d", d=D)
                    nc.vector.tensor_copy(vst[:, r, :, 0:D], v_turned).then_inc(s_vh, 1)
                    dve.wait_ge(s_vh, c + 1)
                    nc.vector.tensor_tensor(vst[:, r, :, D + 1:VW], v_turned, vst[:, r, :, 0:D].bitcast(f32),
                                            ALU.subtract).then_inc(s_ev, 1)

                rest_of_x(0, 0)
                chunks(dve, chunk)

            @block.scalar
            def _(act):
                def round_x(c, i, r):
                    act.wait_ge(s_x[r], 16 * i + 16)
                    act.wait_ge(s_mm, UN * c + UN)
                    nc.scalar.activation(xh[:, r, :, :], xt[:, r, :, :], ACT.Copy).then_inc(s_xh, 1)

                def chunk(c, i, r, prepare):
                    for g in range(NG):
                        act.wait_ge(s_mm, UN * c + MM0 + 2 + g)
                        act.wait_ge(s_q[g % 2], 32 * (NG // 2) * c + 32 * (g // 2) + 32)
                        nc.scalar.activation(qhi[:, g % 2, :], psum[:, 1 + g, :], ACT.Copy).then_inc(s_hi, 1)
                        if g == NG // 2 - 1 and prepare:
                            round_x(c + 1, i + r, 1 - r)

                act.sem_inc(s_mm, MM0)
                round_x(0, 0, 0)
                chunks(act, chunk)

    def attention():
        NQ = 2 * QT
        steps = [(Q, s, 2 * s, min(2, Q % QT + 1 - 2 * s)) for Q in range(NQ) for s in range((Q % QT + 2) // 2)]
        NS = len(steps)
        LAG = 3
        RING = 4
        chunk_width = lambda Q, c: min(CH, Q % QT * P + P - c * CH)
        last_step = {t[0]: n for n, t in enumerate(steps)}

        def max_units(Q):
            events = []
            for c in range((Q % QT * P + P + CH - 1) // CH):
                heads = min(HG, CH // chunk_width(Q, c))
                events += [("max", Q, h, c, heads) for h in range(0, HG, heads)]
            return events

        ahead = max_units(0) + [("shift", 0)] + max_units(1)
        after = []
        for n, (Q, s, _, _) in enumerate(steps):
            ns = (Q % QT + 2) // 2
            todo = max_units(Q + 2) if Q + 2 < NQ else []
            side = [("shift", Q + 1)] if s == min(1, ns - 1) and Q + 1 < NQ else []
            side += todo[len(todo) * s // ns:len(todo) * (s + 1) // ns]
            side += [("turn", q) for q in range(NQ) if last_step[q] + LAG + 2 == n]
            after.append(side)
        tail = [("turn", q) for q in range(NQ) if last_step[q] + LAG + 2 >= NS]
        order = ahead + [e for side in after for e in side] + tail
        NA = len(order)
        index = {e: n for n, e in enumerate(order)}
        by_pool = [n for n in range(NS) if n % 2 == 1]
        by_dve = [n for n in range(NS) if n % 2 == 0]
        assert NA % 2 == 0 and NS % 3 == 0 and NS % RING == 0
        ROUNDS = NU // 2
        PIECES = NSPLIT // ROUNDS
        assert NSPLIT % ROUNDS == 0
        CUTS = 4

        with ExitStack() as st:
            qs = [sb(st, f"qs{r}", [SR + 1, HG, T], f32r) for r in range(2)]
            ks = [sb(st, f"ks{r}", [SR + 1, T], f32r) for r in range(2)]
            vs = [sb(st, f"vs{r}", [P, QT, VW], f32r) for r in range(2)]
            probs = sb(st, "probs", [P, 3, 2, HG * P])
            phi = sb(st, "phi", [P, RING, 2, HG * P], f32r)
            plo = sb(st, "plo", [P, RING, 2, HG * P], f32r)
            o_t = sb(st, "o_t", [VW, 2, HG * P])
            attn = [sb(st, f"attn{r}", [P, QT, HG, D]) for r in range(2)]
            mparts = sb(st, "mparts", [P, 2, HG, T // CH])
            mfull = sb(st, "mfull", [P, 2, HG])
            mrow = sb(st, "mrow", [HG, 2, P], f32r)
            raw = sb(st, "raw", [P, SPLIT])
            whi = sb(st, "whi", [P, SPLIT], f32r)
            wlo = sb(st, "wlo", [P, SPLIT], f32r)
            rden = sb(st, "rden", [P, 2, HG, 1])
            olo = sb(st, "olo", [P, 2, HG, D])
            osum = sb(st, "osum", [P, 2, HG, D])
            s_ld = [sem(st, f"s2_ld{r}") for r in range(2)]
            s_side, s_read = sem(st, "s2_side"), sem(st, "s2_read")
            s_sc, s_ex, s_hi = sem(st, "s2_sc"), sem(st, "s2_ex"), sem(st, "s2_hi")
            s_lod, s_lop, s_pv, s_oc = sem(st, "s2_lod"), sem(st, "s2_lop"), sem(st, "s2_pv"), sem(st, "s2_oc")
            s_mf, s_row, s_turn = sem(st, "s2_mf"), sem(st, "s2_row"), sem(st, "s2_turn")
            s_at = [sem(st, f"s2_at{r}") for r in range(2)]
            s_wl, s_ws, s_wst = sem(st, "s2_wl"), sem(st, "s2_ws"), sem(st, "s2_wst")
            block = st.enter_context(nc.Block())
            score_bank = lambda n: 2 + 2 * (n % 2)
            out_bank = lambda Q: 6 + Q % 2
            tile_of = lambda Q: (Q // QT, Q % QT)

            def wait_lo(eng, i, n):
                m = n % NS
                mine, s = (by_dve, s_lod) if m in by_dve else (by_pool, s_lop)
                eng.wait_ge(s, (i + (1 if n >= 0 else 0)) * len(mine) + mine.index(m) + 1)

            @block.sync
            def _(sp):
                attn_rows = attn_dram.rearrange("(t p) n -> p t n", p=P)

                def load(i, r):
                    b, g = i // (NG // 2), 2 * (i % (NG // 2)) + r
                    sp.dma_start(ks[r][:, :].bitcast(f32), k_dram[:, ds(b * T, T)]).then_inc(s_ld[r], 16)
                    for row, part in ((0, 0), (D, 1), (2 * D, 0)):
                        src = q_dram[part].rearrange("g j d n -> d g j n")[:, ds(g, 1), :, ds(b * T, T)]
                        sp.dma_start(qs[r][row:row + D, :, :].bitcast(f32), src.rearrange("d g j n -> d (g j) n")
                                     ).then_inc(s_ld[r], 16)
                    sp.dma_start(vs[r][:, :, :].bitcast(f32), v_dram[:, ds(b * QT, QT), :]).then_inc(s_ld[r], 16)

                def store(i, r):
                    b, g = i // (NG // 2), 2 * (i % (NG // 2)) + r
                    sp.wait_ge(s_read, i * NA + index[("turn", r * QT + QT - 1)] + 3)
                    sp.dma_start(attn_rows[:, ds(b * QT, QT), ds(g * P, P)],
                                 attn[r][:, :, :, :].rearrange("p t j d -> p t (j d)")).then_inc(s_at[r], 16)

                def round_(i, more):
                    for Q in range(NQ):
                        r, q = tile_of(Q)
                        sp.wait_ge(s_read, i * NA + index[("shift", Q)] + 3)
                        sp.dma_start(qs[r][SR:SR + 1, :, q * P:(q + 1) * P].bitcast(f32),
                                     mrow[:, Q % 2, :].bitcast(f32)).then_inc(s_row, 16)
                        if Q == QT + QT // 2:
                            store(i, 0)
                            if more:
                                load(i + 1, 0)
                    store(i, 1)
                    if more:
                        sp.wait_ge(s_side, (i + 1) * NA + NA)
                        load(i + 1, 1)

                sp.sem_inc(s_at[0], 16)
                sp.sem_inc(s_at[1], 16)
                load(0, 0)
                load(0, 1)
                with sp.Fori(0, ROUNDS - 1) as i:
                    round_(i, True)
                round_(ROUNDS - 1, False)
                for r in range(2):
                    sp.wait_ge(s_at[r], 16 + 16 * ROUNDS)

            @block.tensor
            def _(pe):
                def side(i, e):
                    n = index[e]
                    bank = n % 2
                    Q = e[1]
                    r, q = tile_of(Q)
                    if e[0] == "max":
                        _, _, h0, c, heads = e
                        if q == 0:
                            pe.wait_ge(s_ld[r], 80 * i + 80)
                        pe.wait_ge(s_read, i * NA + n + 1)
                        w = chunk_width(Q, c)
                        diag = c * CH + w == q * P + P
                        for m in range(heads):
                            mm = nc.tensor.matmul(psum[:, bank, m * w:(m + 1) * w],
                                                  qs[r][0:SR, h0 + m, q * P:(q + 1) * P],
                                                  ks[r][0:SR, c * CH:c * CH + w], start=True, stop=not diag)
                            if diag:
                                mm = nc.tensor.matmul(psum[:, bank, (m + 1) * w - P:(m + 1) * w], identb[:, :],
                                                      mask_q[:, :], start=False, stop=True)
                    elif e[0] == "shift":
                        pe.wait_ge(s_read, i * NA + n + 1)
                        pe.wait_ge(s_mf, i * NQ + Q + 1)
                        mm = nc.tensor.transpose(psum[0:HG, bank, 0:P], mfull[:, Q % 2, :], ident[:, :])
                    else:
                        pe.wait_ge(s_read, i * NA + n + 1)
                        pe.wait_ge(s_oc, i * NQ + Q + 3)
                        for h in range(HG):
                            mm = nc.tensor.transpose(psum[:, bank, h * VW:(h + 1) * VW],
                                                     o_t[:, Q % 2, h * P:(h + 1) * P], ident[0:VW, 0:VW])
                    mm.then_inc(s_side, 1)

                def scores(i, n):
                    Q, s, j0, nj = steps[n]
                    r, q = tile_of(Q)
                    if s == 0:
                        pe.wait_ge(s_row, 16 * NQ * i + 16 * Q + 16)
                    pe.wait_ge(s_ex, i * NS + n + 1)
                    for jj in range(nj):
                        j = j0 + jj
                        o = psum[:, score_bank(n) + jj, :]
                        mm = nc.tensor.matmul(o, ks[r][:, j * P:(j + 1) * P], qs[r][:, :, q * P:(q + 1) * P],
                                              start=True, stop=(j != q))
                        if j == q:
                            mm = nc.tensor.matmul(o, identb[:, :], mask_k[:, :, :], start=False, stop=True)
                    mm.then_inc(s_sc, 1)

                def values(i, n):
                    Q, s, j0, nj = steps[n]
                    r, q = tile_of(Q)
                    wait_lo(pe, i, n)
                    if s == 0:
                        pe.wait_ge(s_oc, i * NQ + Q + 1)
                    for jj in range(nj):
                        j = j0 + jj
                        for part in (phi, plo):
                            mm = nc.tensor.matmul(psum[0:VW, out_bank(Q), :], vs[r][:, j, :], part[:, n % RING, jj, :],
                                                  start=(j == 0 and part is phi), stop=(j == q and part is plo))
                    mm.then_inc(s_pv, 1)

                with pe.Fori(0, ROUNDS) as i:
                    for e in ahead:
                        side(i, e)
                    for n in range(NS):
                        scores(i, n)
                        half = len(after[n]) // 2
                        for e in after[n][:half]:
                            side(i, e)
                        if n >= LAG:
                            values(i, n - LAG)
                        for e in after[n][half:]:
                            side(i, e)
                    for n in range(NS - LAG, NS):
                        values(i, n)
                    for e in tail:
                        side(i, e)

            @block.scalar
            def _(act):
                def copy_out(i, Q):
                    act.wait_ge(s_pv, i * NS + last_step[Q] + RING + 1)
                    n = index[("turn", Q - 2)] + NA if Q >= 2 else index[("turn", NQ - 2 + Q)]
                    act.wait_ge(s_side, i * NA + n + 1)
                    nc.scalar.activation(o_t[:, Q % 2, :], psum[0:VW, out_bank(Q), :], ACT.Copy).then_inc(s_oc, 1)

                def exps(i, n):
                    nj = steps[n][3]
                    act.wait_ge(s_sc, i * NS + n + 1)
                    wait_lo(act, i, n - 3)
                    nc.scalar.activation(probs[:, n % 3, 0:nj, :], psum[:, score_bank(n):score_bank(n) + nj, :],
                                         ACT.Exp, scale=SCALE).then_inc(s_ex, 1)

                def round_probs(i, n):
                    nj = steps[n][3]
                    act.wait_ge(s_ex, i * NS + n + 3)
                    act.wait_ge(s_pv, i * NS + n + 1)
                    nc.scalar.activation(phi[:, n % RING, 0:nj, :], probs[:, n % 3, 0:nj, :], ACT.Copy
                                         ).then_inc(s_hi, 1)

                act.sem_inc(s_ex, 2)
                act.sem_inc(s_pv, RING)
                act.sem_inc(s_oc, 2)
                act.sem_inc(s_side, NA)
                with act.Fori(0, ROUNDS) as i:
                    for n in range(NS):
                        exps(i, n)
                        round_probs(i, n)
                        for Q in range(NQ):
                            if last_step[Q] + LAG + 1 == n:
                                copy_out(i, Q)
                    for Q in range(NQ):
                        if last_step[Q] + LAG + 1 >= NS:
                            copy_out(i, Q)

            def rest_of_probs(eng, i, n, done):
                nj = steps[n][3]
                eng.tensor_tensor(plo[:, n % RING, 0:nj, :], probs[:, n % 3, 0:nj, :],
                                  phi[:, n % RING, 0:nj, :].bitcast(f32), ALU.subtract).then_inc(done, 1)

            @block.gpsimd
            def _(pool):
                pool.sem_inc(s_lop, len(by_pool))
                pool.sem_inc(s_ws, 2 * CUTS)

                def load_piece(n):
                    wait_alone(pool, s_ws, 2 * CUTS * n + 2 * CUTS)
                    pool.dma_start(raw[:, :], w_all[:, ds(n * SPLIT, SPLIT)]).then_inc(s_wl, 16)

                def split_piece(n, m):
                    if m == 0:
                        wait_alone(pool, s_wl, 16 * n + 16)
                    if m == CUTS:
                        wait_alone(pool, s_ws, 2 * CUTS * n + 3 * CUTS)
                    c = slice(m % CUTS * (SPLIT // CUTS), (m % CUTS + 1) * (SPLIT // CUTS))
                    if m < CUTS:
                        pool.tensor_copy(whi[:, c], raw[:, c]).then_inc(s_ws, 1)
                    else:
                        pool.tensor_tensor(wlo[:, c], raw[:, c], whi[:, c].bitcast(f32), ALU.subtract
                                           ).then_inc(s_ws, 1)

                def store_piece(n):
                    wait_alone(pool, s_ws, 2 * CUTS * n + 4 * CUTS)
                    pool.dma_start(w_dram[0, :, ds(n * SPLIT, SPLIT)], whi[:, :].bitcast(f32)).then_inc(s_wst, 16)
                    pool.dma_start(w_dram[1, :, ds(n * SPLIT, SPLIT)], wlo[:, :].bitcast(f32)).then_inc(s_wst, 16)

                def stored_piece(n):
                    wait_alone(pool, s_wst, 32 * n + 32)

                stages = ([load_piece] + [lambda n, m=m: split_piece(n, m) for m in range(2 * CUTS)] +
                          [store_piece, stored_piece])
                assert PIECES * len(stages) <= len(by_pool)
                gap = len(by_pool) // (PIECES * len(stages))
                with pool.Fori(0, ROUNDS) as i:
                    for m, n in enumerate(by_pool):
                        wait_alone(pool, s_hi, i * NS + n + 1)
                        rest_of_probs(nc.gpsimd, i, n, s_lop)
                        if m % gap == 0 and m // gap < PIECES * len(stages):
                            stages[m // gap % len(stages)](i * PIECES + m // gap // len(stages))

            @block.vector
            def _(dve):
                def side(i, e):
                    n = index[e]
                    bank = n % 2
                    Q = e[1]
                    r, q = tile_of(Q)
                    dve.wait_ge(s_side, i * NA + NA + n + 1)
                    if e[0] == "max":
                        _, _, h0, c, heads = e
                        w = chunk_width(Q, c)
                        nc.vector.reduce_max(mparts[:, Q % 2, h0:h0 + heads, c],
                                             psum[:, bank, 0:heads * w].rearrange("p (h w) -> p h w", w=w), axis=AX.X
                                             ).then_inc(s_read, 1)
                        if e == max_units(Q)[-1]:
                            dve.wait_ge(s_read, i * NA + n + 3)
                            nc.vector.reduce_max(mfull[:, Q % 2, :], mparts[:, Q % 2, :, 0:c + 1], axis=AX.X
                                                 ).then_inc(s_mf, 1)
                    elif e[0] == "shift":
                        nc.vector.tensor_scalar(mrow[:, Q % 2, :], psum[0:HG, bank, 0:P], -1.0, None, ALU.mult
                                                ).then_inc(s_read, 1)
                    else:
                        if q == 0:
                            dve.wait_ge(s_at[r], 16 * i + 16)
                        turned = psum[:, bank, 0:HG * VW].rearrange("p (h v) -> p h v", v=VW)
                        nc.vector.reciprocal(rden[:, Q % 2, :, :], turned[:, :, D:D + 1]).then_inc(s_turn, 1)
                        nc.vector.tensor_copy(olo[:, Q % 2, :, :], turned[:, :, D + 1:VW]).then_inc(s_turn, 1)
                        dve.wait_ge(s_turn, 3 * NQ * i + 3 * Q + 2)
                        nc.vector.tensor_tensor(osum[:, Q % 2, :, :], turned[:, :, 0:D], olo[:, Q % 2, :, :], ALU.add
                                                ).then_inc(s_turn, 1)
                        dve.wait_ge(s_turn, 3 * NQ * i + 3 * Q + 3)
                        nc.vector.tensor_tensor(attn[r][:, q, :, :], osum[:, Q % 2, :, :],
                                                rden[:, Q % 2, :, :].to_broadcast([P, HG, D]),
                                                ALU.mult).then_inc(s_read, 1)

                def rest(i, n):
                    if n in by_dve:
                        dve.wait_ge(s_hi, i * NS + n + 1)
                        rest_of_probs(nc.vector, i, n, s_lod)

                dve.sem_inc(s_read, 2)
                dve.sem_inc(s_lod, len(by_dve))
                with dve.Fori(0, ROUNDS) as i:
                    for e in ahead:
                        side(i, e)
                    for n in range(NS):
                        half = len(after[n]) // 2
                        for e in after[n][:half]:
                            side(i, e)
                        if n >= 1:
                            rest(i, n - 1)
                        for e in after[n][half:]:
                            side(i, e)
                    rest(i, NS - 1)
                    for e in tail:
                        side(i, e)

    def post_attention():
        with ExitStack() as st:
            wo = sb(st, "wo", [P, KC, HID])
            gw = sb(st, "gw", [P, KC, NE])
            at = sb(st, "at3", [P, 2, HID])
            xs = sb(st, "xs3", [P, 2, HID])
            att = sb(st, "att3", [P, 2, KC, P])
            xt = sb(st, "xt3", [P, 2, KC, P])
            y = sb(st, "y3", [P, 2, HID])
            x1 = sb(st, "x13", [P, 2, HID])
            stats = sb(st, "stats3", [P, 2, 6])
            mv = sb(st, "mv3", [P, 2, 2])
            std = sb(st, "std3", [P, 2])
            rstd = sb(st, "rstd3", [P, 2])
            s_w = sem(st, "s3_w")
            s_ld = [sem(st, f"s3_ld{r}") for r in range(2)]
            s_st = [sem(st, f"s3_st{r}") for r in range(2)]
            s_ta, s_ac, s_pr, s_y = sem(st, "s3_ta"), sem(st, "s3_ac"), sem(st, "s3_pr"), sem(st, "s3_y")
            s_x1, s_tx, s_xc, s_g, s_gc = (sem(st, "s3_x1"), sem(st, "s3_tx"), sem(st, "s3_xc"), sem(st, "s3_g"),
                                           sem(st, "s3_gc"))
            s_ln, s_var, s_std = sem(st, "s3_ln"), sem(st, "s3_var"), sem(st, "s3_std")
            block = st.enter_context(nc.Block())

            @block.sync
            def _(sp):
                sp.dma_start(wo[:, :, :], wo_t.rearrange("(c p) n -> p c n", p=P)).then_inc(s_w, 16)
                sp.dma_start(gw[:, :, :], gate_w.rearrange("(c p) n -> p c n", p=P)).then_inc(s_w, 16)
                def load(t, r):
                    sp.wait_ge(s_y, t + 1)
                    sp.dma_start(at[:, r, :], attn_dram[ds(t * P, P), :]).then_inc(s_ld[r], 16)
                    sp.dma_start(xs[:, r, :], x[ds(t * P, P), :]).then_inc(s_ld[r], 16)

                def store(t, r):
                    sp.wait_ge(s_x1, t + 1)
                    sp.dma_start(x1_dram[ds(t * P, P), :], x1[:, r, :]).then_inc(s_st[r], 16)

                sp.sem_inc(s_st[0], 16)
                sp.sem_inc(s_st[1], 16)
                load(0, 0)
                load(1, 1)
                with sp.Fori(0, NT // 2 - 1) as i:
                    for r in range(2):
                        load(2 * i + 2 + r, r)
                        store(2 * i + r, r)
                store(NT - 2, 0)
                store(NT - 1, 1)
                for r in range(2):
                    sp.wait_ge(s_st[r], 16 + 16 * (NT // 2))

            @block.tensor
            def _(pe):
                def project(t, i, r):
                    pe.wait_ge(s_ld[r], 32 * i + 32)
                    pe.wait_ge(s_ac, t + 1)
                    for k in range(KC):
                        mm = nc.tensor.transpose(psum[:, 0, k * P:(k + 1) * P], at[:, r, k * P:(k + 1) * P], ident[:, :])
                    mm.then_inc(s_ta, 1)
                    pe.wait_ge(s_ac, t + 2)
                    pe.wait_ge(s_y, t + 2)
                    for k in range(KC):
                        mm = nc.tensor.matmul(psum[:, 1, :], att[:, r, k, :], wo[:, k, :],
                                              start=(k == 0), stop=(k == KC - 1))
                    mm.then_inc(s_pr, 1)

                def gate(t, i, r):
                    pe.wait_ge(s_x1, t + 1)
                    pe.wait_ge(s_xc, t + 1)
                    for k in range(KC):
                        mm = nc.tensor.transpose(psum[:, 2, k * P:(k + 1) * P], x1[:, r, k * P:(k + 1) * P], ident[:, :])
                    mm.then_inc(s_tx, 1)
                    pe.wait_ge(s_xc, t + 2)
                    pe.wait_ge(s_gc, t + 1)
                    for k in range(KC):
                        mm = nc.tensor.matmul(psum[:, 3, 0:NE], xt[:, r, k, :], gw[:, k, :],
                                              start=(k == 0), stop=(k == KC - 1))
                    mm.then_inc(s_g, 1)

                pe.wait_ge(s_w, 32)
                project(0, 0, 0)
                with pe.Fori(0, NT // 2 - 1) as i:
                    for r in range(2):
                        t = 2 * i + r
                        project(t + 1, i + r, 1 - r)
                        gate(t, i, r)
                project(NT - 1, NT // 2 - 1, 1)
                gate(NT - 2, NT // 2 - 1, 0)
                gate(NT - 1, NT // 2 - 1, 1)

            @block.scalar
            def _(act):
                def copy_attention(t, r):
                    act.wait_ge(s_ta, t + 1)
                    nc.scalar.activation(att[:, r, :, :].rearrange("p c n -> p (c n)"), psum[:, 0, :], ACT.Copy
                                         ).then_inc(s_ac, 1)

                def copy_x1(t, r):
                    act.wait_ge(s_tx, t + 1)
                    nc.scalar.activation(xt[:, r, :, :].rearrange("p c n -> p (c n)"), psum[:, 2, :], ACT.Copy
                                         ).then_inc(s_xc, 1)

                def root(t, r):
                    act.wait_ge(s_var, t + 1)
                    nc.scalar.activation(std[:, r:r + 1], mv[:, r, 1:2], ACT.Sqrt).then_inc(s_std, 1)

                act.sem_inc(s_ac, 1)
                act.sem_inc(s_xc, 1)
                copy_attention(0, 0)
                root(0, 0)
                with act.Fori(0, NT // 2 - 1) as i:
                    for r in range(2):
                        t = 2 * i + r
                        copy_attention(t + 1, 1 - r)
                        copy_x1(t, r)
                        root(t + 1, 1 - r)
                copy_attention(NT - 1, 1)
                copy_x1(NT - 2, 0)
                root(NT - 1, 1)
                copy_x1(NT - 1, 1)

            @block.vector
            def _(dve):
                def norm(t, i, r):
                    dve.wait_ge(s_pr, t + 1)
                    nc.vector.tensor_tensor(y[:, r, :], psum[:, 1, :], xs[:, r, :], ALU.add).then_inc(s_y, 1)
                    dve.wait_ge(s_y, t + 3)
                    nc.vector.bn_stats(stats[:, r, :], y[:, r, :]).then_inc(s_ln, 1)
                    wait_alone(dve, s_ln, 3 * t + 1)
                    nc.vector.bn_aggr(mv[:, r, :], stats[:, r, :]).then_inc(s_ln, 1)
                    dve.wait_ge(s_ln, 3 * t + 2)
                    nc.vector.tensor_scalar(mv[:, r, 1:2], mv[:, r, 1:2], EPS, None, ALU.add).then_inc(s_var, 1)
                    dve.wait_ge(s_std, t + 1)
                    nc.vector.reciprocal(rstd[:, r:r + 1], std[:, r:r + 1]).then_inc(s_ln, 1)
                    dve.wait_ge(s_ln, 3 * t + 3)
                    dve.wait_ge(s_st[r], 16 * i + 16)
                    nc.vector.tensor_scalar(x1[:, r, :], y[:, r, :], mv[:, r, 0:1], rstd[:, r:r + 1],
                                            ALU.subtract, ALU.mult).then_inc(s_x1, 1)

                def keep_logits(t):
                    dve.wait_ge(s_g, t + 1)
                    nc.vector.tensor_copy(logits[:, ds(t, 1), :].rearrange("p t e -> p (t e)"),
                                          psum[:, 3, 0:NE]).then_inc(s_gc, 1)

                dve.sem_inc(s_y, 2)
                dve.sem_inc(s_gc, 1)
                norm(0, 0, 0)
                with dve.Fori(0, NT // 2 - 1) as i:
                    for r in range(2):
                        t = 2 * i + r
                        norm(t + 1, i + r, 1 - r)
                        keep_logits(t)
                norm(NT - 1, NT // 2 - 1, 1)
                keep_logits(NT - 2)
                keep_logits(NT - 1)

    def expert_tiles(st, name, n_tiles, shared, block, xin, ybuf, score_of, weights_of, s_ld, s_used, s_y, s_st,
                     residual=None):
        xh = sb(st, name + "_xh", [P, KC, P], f32r)
        xl = sb(st, name + "_xl", [P, KC, P], f32r)
        gact = sb(st, name + "_g", [P, F])
        h = sb(st, name + "_h", [P, F])
        hh = sb(st, name + "_hh", [FP, KC, P], f32r)
        hl = sb(st, name + "_hl", [FP, KC, P], f32r)
        names = ("xhi", "xlo", "up", "silu", "h", "th", "hhi", "hlo", "dn")
        s = {n: sem(st, f"{name}_{n}") for n in names}
        XB, UB, GB, HB, YB = 0, 1, 2, 3, 4
        out_done = s["dn"]

        @block.tensor
        def _(pe):
            def turn_x(t, i, r):
                pe.wait_ge(s_ld[r], 16 * i + 16)
                for k in range(KC):
                    mm = nc.tensor.transpose(psum[:, XB, k * P:(k + 1) * P], xin[:, r, k * P:(k + 1) * P], ident[:, :])
                mm.then_inc(s_used, 1)

            def up(t):
                w = weights_of(pe, t, True)
                pe.wait_ge(s["xlo"], t + 1)
                for bank, col in ((UB, 0), (GB, W3)):
                    for k in range(KC):
                        for n, (a, part) in enumerate(((xh, 0), (xh, 1), (xl, 0))):
                            mm = nc.tensor.matmul(psum[:, bank, 0:F], a[:, k, :], w(P, part, col + k * F, F),
                                                  start=(k == 0 and n == 0), stop=(k == KC - 1 and n == 2))
                mm.then_inc(s["up"], 1)

            def turn_h(t):
                pe.wait_ge(s["h"], t + 1)
                for k in range(KC):
                    mm = nc.tensor.transpose(psum[0:FP, HB, k * P:(k + 1) * P], h[:, k * FP:(k + 1) * FP], ident[:, :])
                mm.then_inc(s["th"], 1)

            def down(t, w):
                pe.wait_ge(s["hlo"], t + 1)
                pe.wait_ge(s_y, t + 1)
                for k in range(KC):
                    for n, (a, part) in enumerate(((hh, 0), (hh, 1), (hl, 0))):
                        mm = nc.tensor.matmul(psum[:, YB, :], a[:, k, :], w(FP, part, W2 + k * HID, HID),
                                              start=(k == 0 and n == 0), stop=(k == KC - 1 and n == 2))
                mm.then_inc(s["dn"], 1)

            pe.sem_inc(s["dn"], 1)
            turn_x(0, 0, 0)
            up(0)
            turn_x(1, 0, 1)
            turn_h(0)
            with pe.Fori(0, n_tiles // 2 - 1) as i:
                for r in range(2):
                    t = 2 * i + 1 + r
                    up(t)
                    turn_x(t + 1, i + 1, r)
                    down(t - 1, weights_of(pe, t - 1, False))
                    turn_h(t)
            t = n_tiles - 1
            up(t)
            down(t - 1, weights_of(pe, t - 1, False))
            turn_h(t)
            down(t, weights_of(pe, t, False))

        @block.scalar
        def _(act):
            def silu(t):
                act.wait_ge(s["up"], t + 1)
                nc.scalar.activation(gact[:, :], psum[:, UB, 0:F], ACT.Silu, scale=score_of(t)).then_inc(s["silu"], 1)

            def split_x(t):
                act.wait_ge(s_used, t + 3)
                nc.scalar.activation(xh[:, :, :].rearrange("p c n -> p (c n)"), psum[:, XB, :], ACT.Copy
                                     ).then_inc(s["xhi"], 1)

            def split_h(t):
                act.wait_ge(s["th"], t + 1)
                nc.scalar.activation(hh[:, :, :].rearrange("p c n -> p (c n)"), psum[0:FP, HB, :], ACT.Copy
                                     ).then_inc(s["hhi"], 1)

            def store_ready(t, i, r):
                if shared:
                    return
                act.wait_ge(s["dn"], t + 2)
                act.wait_ge(s_st[r], 16 * i + 16)
                nc.scalar.activation(ybuf[:, r, :], psum[:, YB, :], ACT.Copy).then_inc(s_y, 1)

            split_x(0)
            silu(0)
            split_x(1)
            split_h(0)
            with act.Fori(0, n_tiles // 2 - 1) as i:
                for r in range(2):
                    t = 2 * i + 1 + r
                    silu(t)
                    split_x(t + 1)
                    store_ready(t - 1, i, r)
                    split_h(t)
            t = n_tiles - 1
            silu(t)
            store_ready(t - 1, n_tiles // 2 - 1, 0)
            split_h(t)
            store_ready(t, n_tiles // 2 - 1, 1)

        @block.vector
        def _(dve):
            def gated(t):
                dve.wait_ge(s["silu"], t + 1)
                nc.vector.scalar_tensor_tensor(out=h[:, :], in0=psum[:, GB, 0:F], scalar=score_of(t), in1=gact[:, :],
                                               op0=ALU.mult, op1=ALU.mult).then_inc(s["h"], 1)

            def rest_x(t):
                dve.wait_ge(s["xhi"], t + 1)
                nc.vector.tensor_tensor(xl[:, :, :].rearrange("p c n -> p (c n)"), psum[:, XB, :],
                                        xh[:, :, :].rearrange("p c n -> p (c n)").bitcast(f32), ALU.subtract
                                        ).then_inc(s["xlo"], 1)

            def rest_h(t):
                dve.wait_ge(s["hhi"], t + 1)
                nc.vector.tensor_tensor(hl[:, :, :].rearrange("p c n -> p (c n)"), psum[0:FP, HB, :],
                                        hh[:, :, :].rearrange("p c n -> p (c n)").bitcast(f32), ALU.subtract
                                        ).then_inc(s["hlo"], 1)

            def add_residual(t, i, r):
                if not shared:
                    return
                dve.wait_ge(s["dn"], t + 2)
                dve.wait_ge(residual[r], 16 * i + 16)
                nc.vector.tensor_tensor(ybuf[:, r, :], psum[:, YB, :], ybuf[:, r, :], ALU.add).then_inc(s_y, 1)

            rest_x(0)
            gated(0)
            rest_x(1)
            rest_h(0)
            with dve.Fori(0, n_tiles // 2 - 1) as i:
                for r in range(2):
                    t = 2 * i + 1 + r
                    gated(t)
                    rest_x(t + 1)
                    add_residual(t - 1, i, r)
                    rest_h(t)
            t = n_tiles - 1
            gated(t)
            add_residual(t - 1, n_tiles // 2 - 1, 0)
            rest_h(t)
            add_residual(t, n_tiles // 2 - 1, 1)

        return out_done

    def experts():
        NK = NT * TOPK
        with ExitStack() as outer:
            wbuf = sb(outer, "wbuf", [P, 2 * 2 * WW], f32r)
            table = sb(outer, "table", [1, 5, RT], i32)
            rlist = sb(outer, "rlist", [P, 2 * RT], i32)
            slot = sb(outer, "slot", [P, NK], i32)
            entry = sb(outer, "entry", [P, NK, 2], i32)
            s_wl = sem(outer, "s5_wl")

            def routing():
                with ExitStack() as st:
                    names3 = ("shifted", "expd", "score", "biased", "eq", "cand", "oh0", "oh1", "prod", "tot",
                              "incl", "posf")
                    a = {n: sb(st, "r_" + n, [P, NT, NE]) for n in names3}
                    row = {n: sb(st, "r_" + n, [P, NT, 1]) for n in ("mx", "sum", "inv", "best", "first", "p0", "p1",
                                                                     "tokf")}
                    ex = {n: sb(st, "r_" + n, [P, 1, NE]) for n in ("bias", "iota", "nt", "tsi", "ts",
                                                                    "base", "one8")}
                    tb = {n: sb(st, "r_" + n, [1, RT, NE]) for n in ("ge", "eqt")}
                    te = {n: sb(st, "r_" + n, [1, RT, 1]) for n in ("e", "flag", "iota_t")}
                    cnt_i = sb(st, "r_cnt_i", [P, 1, NE], i32)
                    lane_i = sb(st, "r_lane_i", [P, NT], i32)
                    tile_i = sb(st, "r_tile_i", [P, NT], i32)
                    half_i = sb(st, "r_half_i", [1, RT, 1], i32)
                    tri = sb(st, "r_tri", [P, P])
                    ones = sb(st, "r_ones", [P, P])
                    s_c, s_step, s_exp, s_m, s_cnt = (sem(st, "s4_c"), sem(st, "s4_step"), sem(st, "s4_exp"),
                                                      sem(st, "s4_m"), sem(st, "s4_cnt"))
                    s_in = sem(st, "s4_in")
                    block = st.enter_context(nc.Block())

                    @block.sync
                    def _(sp):
                        sp.dma_start(ex["bias"][:, 0, :], expert_bias).then_inc(s_in, 16)
                        sp.dma_start(ex["iota"][:, 0, :], c_expert).then_inc(s_in, 16)
                        sp.dma_start(row["tokf"][:, :, 0], c_token).then_inc(s_in, 16)
                        sp.dma_start(te["iota_t"][:, :, 0], c_tile).then_inc(s_in, 16)
                        sp.dma_start(tri[:, :], c_tri).then_inc(s_in, 16)

                    @block.scalar
                    def _(act):
                        act.wait_ge(s_exp, 1)
                        nc.scalar.activation(a["expd"][:, :, :], a["shifted"][:, :, :], ACT.Exp).then_inc(s_exp, 1)

                    @block.tensor
                    def _(pe):
                        pe.wait_ge(s_m, 1)
                        flat = a["prod"][:, :, :].rearrange("p t e -> p (t e)")
                        nc.tensor.matmul(psum[:, 0, 0:NT * NE], tri[:, :], flat, start=True, stop=True)
                        nc.tensor.matmul(psum[:, 1, 0:NT * NE], ones[:, :], flat, start=True, stop=True
                                         ).then_inc(s_cnt, 1)

                    @block.vector
                    def _(dve):
                        steps_done = [0]

                        def then(ins):
                            steps_done[0] += 1
                            ins.then_inc(s_step, 1)
                            dve.wait_ge(s_step, steps_done[0])

                        v = nc.vector
                        TE = [P, NT, NE]
                        then(v.memset(ones[:, :], 1.0))
                        then(v.memset(ex["one8"][:, :, :], 1.0))
                        then(v.reduce_max(row["mx"][:, :, 0], logits[:, :, :], axis=AX.X))
                        then(v.tensor_tensor(a["shifted"][:, :, :], logits[:, :, :],
                                             row["mx"][:, :, :].to_broadcast(TE), ALU.subtract))
                        dve.sem_inc(s_exp, 1)
                        dve.wait_ge(s_exp, 2)
                        then(v.reduce_sum(row["sum"][:, :, 0], a["expd"][:, :, :], axis=AX.X))
                        then(v.reciprocal(row["inv"][:, :, :], row["sum"][:, :, :]))
                        then(v.tensor_tensor(a["score"][:, :, :], a["expd"][:, :, :],
                                             row["inv"][:, :, :].to_broadcast(TE), ALU.mult))
                        dve.wait_ge(s_in, 80)
                        then(v.tensor_tensor(a["biased"][:, :, :], a["score"][:, :, :],
                                             ex["bias"][:, :, :].to_broadcast(TE), ALU.add))
                        entries = entry[:, :, :].rearrange("p (t k) e -> p t k e", k=TOPK)
                        for k, oh in enumerate(("oh0", "oh1")):
                            then(v.reduce_max(row["best"][:, :, 0], a["biased"][:, :, :], axis=AX.X))
                            then(v.tensor_tensor(a["eq"][:, :, :], a["biased"][:, :, :],
                                                 row["best"][:, :, :].to_broadcast(TE), ALU.is_equal))
                            then(v.scalar_tensor_tensor(out=a["cand"][:, :, :], in0=a["eq"][:, :, :],
                                                        scalar=-float(NE), in1=ex["iota"][:, :, :].to_broadcast(TE),
                                                        op0=ALU.mult, op1=ALU.add))
                            then(v.tensor_reduce(row["first"][:, :, 0], a["cand"][:, :, :], axis=AX.X, op=ALU.min))
                            then(v.tensor_tensor(a[oh][:, :, :], a["cand"][:, :, :],
                                                 row["first"][:, :, :].to_broadcast(TE), ALU.is_equal))
                            then(v.scalar_tensor_tensor(out=a["biased"][:, :, :], in0=a[oh][:, :, :], scalar=MASKED,
                                                        in1=a["biased"][:, :, :], op0=ALU.mult, op1=ALU.add))
                            then(v.tensor_tensor(a["eq"][:, :, :], a[oh][:, :, :], a["score"][:, :, :], ALU.mult))
                            then(v.reduce_sum(entries[:, :, k, 1].bitcast(f32), a["eq"][:, :, :], axis=AX.X))
                            then(v.tensor_copy(entries[:, :, k, 0], row["tokf"][:, :, 0]))
                        then(v.tensor_tensor(a["prod"][:, :, :], a["oh0"][:, :, :], a["oh1"][:, :, :], ALU.add))
                        dve.sem_inc(s_m, 1)
                        dve.wait_ge(s_cnt, 1)
                        then(v.tensor_copy(a["tot"][:, :, :],
                                           psum[:, 1, 0:NT * NE].rearrange("p (t e) -> p t e", e=NE)))
                        for e in range(NE):
                            then(v.tensor_tensor_scan(a["incl"][:, :, e], ones[:, 0:NT], a["tot"][:, :, e], 0.0,
                                                      ALU.mult, ALU.add))
                        cnt = a["incl"][:, NT - 1:NT, :]
                        then(v.tensor_scalar(cnt_i[:, :, :], cnt, float(P - 1), None, ALU.add))
                        then(v.tensor_scalar(cnt_i[:, :, :], cnt_i[:, :, :], PLOG, None, ALU.logical_shift_right))
                        then(v.tensor_scalar(ex["nt"][:, :, :], cnt_i[:, :, :], 1.0, None, ALU.max))
                        then(v.tensor_tensor_scan(ex["tsi"][:, 0, :], ex["one8"][:, 0, :], ex["nt"][:, 0, :], 0.0,
                                                  ALU.mult, ALU.add))
                        then(v.tensor_tensor(ex["ts"][:, :, :], ex["tsi"][:, :, :], ex["nt"][:, :, :], ALU.subtract))
                        then(v.tensor_scalar(ex["base"][:, :, :], ex["ts"][:, :, :], float(P), None, ALU.mult))
                        then(v.tensor_tensor(a["posf"][:, :, :], a["incl"][:, :, :], a["tot"][:, :, :], ALU.subtract))
                        then(v.tensor_tensor(a["posf"][:, :, :], a["posf"][:, :, :],
                                             ex["base"][:, :, :].to_broadcast(TE), ALU.add))
                        then(v.tensor_tensor(a["posf"][:, :, :],
                                             psum[:, 0, 0:NT * NE].rearrange("p (t e) -> p t e", e=NE),
                                             a["posf"][:, :, :], ALU.add))
                        slots = slot[:, :].rearrange("p (t k) -> p t k", k=TOPK)
                        for k, oh in enumerate(("oh0", "oh1")):
                            p = row[f"p{k}"]
                            then(v.tensor_tensor(a["eq"][:, :, :], a[oh][:, :, :], a["posf"][:, :, :], ALU.mult))
                            then(v.reduce_sum(p[:, :, 0], a["eq"][:, :, :], axis=AX.X))
                            then(v.tensor_copy(pos[:, k, :], p[:, :, 0]))
                            then(v.tensor_scalar(lane_i[:, :], pos[:, k, :], P - 1, None, ALU.bitwise_and))
                            then(v.tensor_scalar(tile_i[:, :], pos[:, k, :], PLOG, None, ALU.logical_shift_right))
                            then(v.scalar_tensor_tensor(out=slots[:, :, k], in0=lane_i[:, :],
                                                        scalar=float(RT), in1=tile_i[:, :],
                                                        op0=ALU.mult, op1=ALU.add))
                        R = [1, RT, NE]
                        it = te["iota_t"][:, :, :].to_broadcast(R)
                        then(v.tensor_tensor(tb["ge"][:, :, :], it, ex["tsi"][0:1, :, :].to_broadcast(R), ALU.is_ge))
                        then(v.reduce_sum(te["e"][:, :, 0], tb["ge"][:, :, :], axis=AX.X))
                        then(v.tensor_scalar(te["e"][:, :, :], te["e"][:, :, :], float(NE - 1), None, ALU.min))
                        then(v.tensor_tensor(tb["eqt"][:, :, :], it, ex["ts"][0:1, :, :].to_broadcast(R), ALU.is_equal))
                        then(v.reduce_sum(te["flag"][:, :, 0], tb["eqt"][:, :, 0:NE - 1], axis=AX.X))
                        then(v.tensor_scalar(half_i[:, :, :], te["e"][:, :, :], 1.0, None, ALU.add))
                        then(v.tensor_scalar(half_i[:, :, :], half_i[:, :, :], 1, None, ALU.bitwise_and))
                        then(v.tensor_scalar(table[:, 0, :], half_i[:, :, 0], 2.0 * WW, None, ALU.mult))
                        then(v.tensor_scalar(table[:, 1, :], te["e"][:, :, 0], 32.0, 64.0, ALU.mult, ALU.add))
                        then(v.tensor_copy(table[:, 2, :], te["flag"][:, :, 0]))
                        then(v.tensor_scalar(table[:, 3, :], te["e"][:, :, 0], float(WW), 2.0 * WW, ALU.mult, ALU.add))
                        then(v.tensor_scalar(table[:, 4, :], half_i[:, :, 0], -2.0 * WW, 2.0 * WW,
                                             ALU.mult, ALU.add))

            def shared_expert():
                with ExitStack() as st:
                    xin = sb(st, "xin5", [P, 2, HID])
                    ybuf = sb(st, "y5", [P, 2, HID])
                    idx = sb(st, "idx5", [P, 16], i32)
                    ent = sb(st, "ent5", [P, 32], i32)
                    s_ld = [sem(st, f"s5_ld{r}") for r in range(2)]
                    s_used, s_y = sem(st, "s5_used"), sem(st, "s5_y")
                    s_st = [sem(st, f"s5_st{r}") for r in range(2)]
                    s_fill = [sem(st, f"s5_fill{r}") for r in range(2)]
                    s_cp, s_sc, s_rl = sem(st, "s5_cp"), sem(st, "s5_sc"), sem(st, "s5_rl")
                    block = st.enter_context(nc.Block())

                    def weights_of(pe, t, first_use):
                        return lambda rows, part, col, width: wbuf[0:rows, part * WW + col:part * WW + col + width]

                    @block.sync
                    def _(sp):
                        for e in range(2):
                            for part in range(2):
                                sp.dma_start(wbuf[:, (2 * e + part) * WW:(2 * e + part + 1) * WW].bitcast(f32),
                                             w_dram[part, :, e * WW:(e + 1) * WW]).then_inc(s_wl, 16)
                            if e == 0:
                                sp.wait_ge(s_wl, 32)

                        def load(t, r):
                            sp.wait_ge(s_used, t + 1)
                            sp.dma_start(xin[:, r, :], x1_dram[ds(t * P, P), :]).then_inc(s_ld[r], 16)

                        def fill(t, i, r):
                            sp.wait_ge(s_st[r], 16 * i + 16)
                            sp.dma_start(ybuf[:, r, :], x1_dram[ds(t * P, P), :]).then_inc(s_fill[r], 16)

                        def store(t, r):
                            sp.wait_ge(s_y, t + 2)
                            sp.dma_start(y_dram[ds(t * P, P), :], ybuf[:, r, :]).then_inc(s_st[r], 16)

                        sp.sem_inc(s_st[0], 16)
                        sp.sem_inc(s_st[1], 16)
                        for r in range(2):
                            load(r, r)
                            fill(r, 0, r)
                        with sp.Fori(0, NT // 2 - 1) as i:
                            for r in range(2):
                                t = 2 * i + r
                                load(t + 2, r)
                                store(t, r)
                                fill(t + 2, i + 1, r)
                        store(NT - 2, 0)
                        store(NT - 1, 1)
                        for r in range(2):
                            sp.wait_ge(s_st[r], 16 + 16 * (NT // 2))
                        sp.wait_ge(s_wl, 64)

                    @block.gpsimd
                    def _(pool):
                        with pool.Fori(0, NK // 16) as m:
                            pool.tensor_copy(idx[:, :], slot[:, ds(16 * m, 16)]).then_inc(s_cp, 1)
                            pool.tensor_copy(ent[:, :], entry[:, :, :].rearrange("p n e -> p (n e)")[:, ds(32 * m, 32)]
                                             ).then_inc(s_cp, 1)
                            wait_alone(pool, s_cp, 2 * m + 2)
                            for n in range(16):
                                pool.indirect_dma_start(
                                    list_dram, bass.IndirectOffsetOnAxis(ap=idx[:, n:n + 1], axis=0),
                                    ent[:, 2 * n:2 * n + 2], None).then_inc(s_sc, 16)
                            wait_alone(pool, s_sc, 256 * m + 256)
                        pool.dma_start(rlist[:, :], list_dram.rearrange("(p t) e -> p (t e)", p=P)).then_inc(s_rl, 16)
                        wait_alone(pool, s_rl, 16)

                    @block.scalar
                    def _(act):
                        act.sem_inc(s_used, 2)
                        act.sem_inc(s_y, 1)

                    @block.tensor
                    def _(pe):
                        pe.wait_ge(s_wl, 32)

                    expert_tiles(st, "e5", NT, True, block, xin, ybuf, lambda t: 1.0, weights_of,
                                 s_ld, s_used, s_y, s_st, residual=s_fill)

            def routed_experts():
                with ExitStack() as st:
                    xin = sb(st, "xin6", [P, 2, HID])
                    ybuf = sb(st, "y6", [P, 2, HID])
                    idx = sb(st, "idx6", [P, 2], i32)
                    s_ld = [sem(st, f"s6_ld{r}") for r in range(2)]
                    s_used, s_y, s_cp = sem(st, "s6_used"), sem(st, "s6_y"), sem(st, "s6_cp")
                    s_st = [sem(st, f"s6_st{r}") for r in range(2)]
                    block = st.enter_context(nc.Block())

                    def weights_of(pe, t, first_use):
                        if first_use:
                            need = pe.value_load(table[0:1, 1, ds(t, 1)], min_val=64, max_val=32 * (NE + 1))
                            wait_alone(pe, s_wl, need)
                        base = pe.value_load(table[0:1, 0, ds(t, 1)], min_val=0, max_val=2 * WW)
                        return lambda rows, part, col, width: wbuf[0:rows, ds(base + part * WW + col, width)]

                    @block.scalar
                    def _(act):
                        act.sem_inc(s_used, 2)
                        act.sem_inc(s_y, 1)

                    done = expert_tiles(st, "e6", RT, False, block, xin, ybuf,
                                        lambda t: rlist[:, ds(2 * t + 1, 1)].bitcast(f32), weights_of,
                                        s_ld, s_used, s_y, s_st)

                    @block.gpsimd
                    def _(pool):
                        with pool.Fori(0, RT // 2) as i:
                            for r in range(2):
                                t = 2 * i + r
                                wait_alone(pool, s_used, t + 1)
                                pool.tensor_copy(idx[:, r:r + 1], rlist[:, ds(2 * t, 1)]).then_inc(s_cp, 1)
                                wait_alone(pool, s_cp, t + 1)
                                pool.indirect_dma_start(xin[:, r, :], None, x1_dram,
                                                        bass.IndirectOffsetOnAxis(ap=idx[:, r:r + 1], axis=0)
                                                        ).then_inc(s_ld[r], 16)

                    @block.sync
                    def _(sp):
                        sp.sem_inc(s_st[0], 16)
                        sp.sem_inc(s_st[1], 16)

                        def next_weights(t):
                            flag = sp.value_load(table[0:1, 2, ds(t, 1)], min_val=0, max_val=1)
                            with sp.If(flag > 0):
                                need = sp.value_load(table[0:1, 1, ds(t, 1)], min_val=64, max_val=32 * (NE + 1))
                                src = sp.value_load(table[0:1, 3, ds(t, 1)], min_val=0, max_val=NE * WW)
                                dst = sp.value_load(table[0:1, 4, ds(t, 1)], min_val=0, max_val=2 * WW)
                                wait_alone(sp, s_wl, need)
                                wait_alone(sp, done, t + 1)
                                for part in range(2):
                                    sp.dma_start(wbuf[:, ds(dst + part * WW, WW)].bitcast(f32),
                                                 w_dram[part, :, ds(src, WW)]).then_inc(s_wl, 16)

                        def store(t, r):
                            sp.wait_ge(s_y, t + 2)
                            sp.dma_start(r_dram[ds(t * P, P), :], ybuf[:, r, :]).then_inc(s_st[r], 16)

                        next_weights(0)
                        with sp.Fori(0, RT // 2 - 1) as i:
                            for r in range(2):
                                t = 2 * i + r
                                next_weights(t + 1)
                                store(t, r)
                        next_weights(RT - 1)
                        store(RT - 2, 0)
                        store(RT - 1, 1)
                        for r in range(2):
                            sp.wait_ge(s_st[r], 16 + 16 * (RT // 2))

            routing()
            shared_expert()
            routed_experts()

    def combine():
        with ExitStack() as st:
            BUFS = 4
            ys = sb(st, "ys7", [P, BUFS, HID])
            g0 = sb(st, "g07", [P, BUFS, HID])
            g1 = sb(st, "g17", [P, BUFS, HID])
            o = sb(st, "o7", [P, BUFS, HID])
            idx = sb(st, "idx7", [P, 2, TOPK, BUFS], i32)
            stats = sb(st, "stats7", [P, BUFS, 6])
            mv = sb(st, "mv7", [P, BUFS, 2])
            std = sb(st, "std7", [P, BUFS])
            rstd = sb(st, "rstd7", [P, BUFS])
            s_ld = [sem(st, f"s7_ld{r}") for r in range(BUFS)]
            s_gt = [sem(st, f"s7_gt{r}") for r in range(BUFS)]
            s_st = [sem(st, f"s7_st{r}") for r in range(BUFS)]
            s_cp, s_ln, s_o = sem(st, "s7_cp"), sem(st, "s7_ln"), sem(st, "s7_o")
            s_var, s_std, s_rstd = sem(st, "s7_var"), sem(st, "s7_std"), sem(st, "s7_rstd")
            assert NT % (2 * BUFS) == 0
            block = st.enter_context(nc.Block())

            @block.sync
            def _(sp):
                with sp.Fori(0, NT // BUFS) as i:
                    for r in range(BUFS):
                        t = BUFS * i + r
                        sp.wait_ge(s_o, t + 1)
                        sp.dma_start(ys[:, r, :], y_dram[ds(t * P, P), :]).then_inc(s_ld[r], 16)

            @block.scalar
            def _(act):
                def root(t, r):
                    act.wait_ge(s_var, t + 1)
                    nc.scalar.activation(std[:, r:r + 1], mv[:, r, 1:2], ACT.Sqrt).then_inc(s_std, 1)

                def store(t, r):
                    act.wait_ge(s_o, t + BUFS + 1)
                    act.dma_start(out[ds(t * P, P), :], o[:, r, :]).then_inc(s_st[r], 16)

                for r in range(BUFS):
                    act.sem_inc(s_st[r], 16)
                act.sem_inc(s_o, BUFS)
                root(0, 0)
                with act.Fori(0, NT // BUFS - 1) as i:
                    for r in range(BUFS):
                        root(BUFS * i + r + 1, (r + 1) % BUFS)
                        store(BUFS * i + r, r)
                for t in range(NT - BUFS, NT):
                    if t + 1 < NT:
                        root(t + 1, (t + 1) % BUFS)
                    store(t, t % BUFS)
                for r in range(BUFS):
                    act.wait_ge(s_st[r], 16 + 16 * (NT // BUFS))

            @block.gpsimd
            def _(pool):
                with pool.Fori(0, NT // (2 * BUFS)) as i:
                    for half in range(2):
                        m = 2 * i + half
                        wait_alone(pool, s_o, BUFS * m + 1)
                        pool.tensor_copy(idx[:, half, :, :], pos[:, :, ds(BUFS * m, BUFS)]).then_inc(s_cp, 1)
                        wait_alone(pool, s_cp, m + 1)
                        for r in range(BUFS):
                            if r > 0:
                                wait_alone(pool, s_o, BUFS * m + r + 1)
                            for k, g in enumerate((g0, g1)):
                                pool.indirect_dma_start(g[:, r, :], None, r_dram,
                                                        bass.IndirectOffsetOnAxis(ap=idx[:, half, k, r:r + 1], axis=0)
                                                        ).then_inc(s_gt[r], 16)

            @block.vector
            def _(dve):
                v = nc.vector
                LN = 4

                def sum_and_moments(t, i, r):
                    dve.wait_ge(s_ld[r], 16 * i + 16)
                    dve.wait_ge(s_gt[r], 32 * i + 32)
                    v.tensor_tensor(g0[:, r, :], g0[:, r, :], g1[:, r, :], ALU.add).then_inc(s_ln, 1)
                    dve.wait_ge(s_ln, LN * t + 1)
                    v.tensor_tensor(ys[:, r, :], ys[:, r, :], g0[:, r, :], ALU.add).then_inc(s_ln, 1)
                    dve.wait_ge(s_ln, LN * t + 2)
                    v.bn_stats(stats[:, r, :], ys[:, r, :]).then_inc(s_ln, 1)
                    wait_alone(dve, s_ln, LN * t + 3)
                    v.bn_aggr(mv[:, r, :], stats[:, r, :]).then_inc(s_ln, 1)
                    dve.wait_ge(s_ln, LN * t + 4)
                    v.tensor_scalar(mv[:, r, 1:2], mv[:, r, 1:2], EPS, None, ALU.add).then_inc(s_var, 1)

                def normalise(t, i, r):
                    dve.wait_ge(s_std, t + 1)
                    v.reciprocal(rstd[:, r:r + 1], std[:, r:r + 1]).then_inc(s_rstd, 1)
                    dve.wait_ge(s_rstd, t + 1)
                    dve.wait_ge(s_st[r], 16 * i + 16)
                    v.tensor_scalar(o[:, r, :], ys[:, r, :], mv[:, r, 0:1], rstd[:, r:r + 1],
                                    ALU.subtract, ALU.mult).then_inc(s_o, 1)

                sum_and_moments(0, 0, 0)
                with dve.Fori(0, NT // BUFS - 1) as i:
                    for r in range(BUFS):
                        sum_and_moments(BUFS * i + r + 1, i + (r + 1) // BUFS, (r + 1) % BUFS)
                        normalise(BUFS * i + r, i, r)
                for t in range(NT - BUFS, NT):
                    if t + 1 < NT:
                        sum_and_moments(t + 1, (t + 1) // BUFS, (t + 1) % BUFS)
                    normalise(t, t // BUFS, t % BUFS)

    with top:
        projections()
        attention()
        post_attention()
        experts()
        combine()


def kernel(**inputs):
    import numpy as np
    import concourse.bacc as bacc
    from concourse import mybir
    from concourse.bass_utils import run_bass_kernel_spmd

    a = {n.replace("L0_", ""): np.asarray(v) for n, v in inputs.items()}
    x = a["attn_hidden_states"]
    B, T, HID = x.shape
    D = a["attn_Wk"].shape[0]
    H = HID // D
    NE, _, F = a["ffn_w1"].shape
    TOPK, P = 2, 128
    N = B * T
    NT, KC = N // P, HID // P
    RT = TOPK * NT + NE
    FP = F // KC

    order = np.concatenate([np.arange(0, D, 2), np.arange(1, D, 2)])
    heads = (np.arange(H)[:, None] * D + order[None, :]).reshape(-1)
    half = D // 2
    theta = (1.0 / 10000.0 ** (np.arange(0, half, 2, dtype=np.float32) / half)).astype(np.float32)
    angle = (np.arange(H, dtype=np.float32)[:, None] * np.tile(theta, 2)[None, :]).astype(np.float32)
    cos = np.ascontiguousarray(np.broadcast_to(np.cos(angle), (P, H, half)), dtype=np.float32)
    sin = np.ascontiguousarray(np.broadcast_to(np.sin(angle), (P, H, half)), dtype=np.float32)

    def expert(w1, w3, w2):
        up = [w.reshape(KC, P, F).transpose(1, 0, 2).reshape(P, KC * F) for w in (w1, w3)]
        down = np.zeros((P, KC, HID), np.float32)
        down[:FP] = w2.reshape(KC, FP, HID).transpose(1, 0, 2)
        return np.concatenate(up + [down.reshape(P, KC * HID)], axis=1)

    w_all = np.concatenate([expert(a["ffn_sw1"], a["ffn_sw3"], a["ffn_sw2"])] +
                           [expert(a["ffn_w1"][e], a["ffn_w3"][e], a["ffn_w2"][e]) for e in range(NE)], axis=1)
    wk_t = a["attn_Wk"][order].T
    arrays = {
        "x": x.reshape(N, HID),
        "x_t": x.reshape(N, HID).T,
        "wq_t": a["attn_Wq"][heads].T,
        "wkv_t": np.concatenate([wk_t, wk_t, wk_t, a["attn_Wv"].T], axis=1),
        "wo_t": a["attn_Wo"].T,
        "rope_cos": cos,
        "rope_sin": sin,
        "gate_w": a["ffn_gate_w"],
        "expert_bias": np.broadcast_to(a["ffn_expert_bias"], (P, NE)),
        "w_all": w_all,
        "c_expert": np.broadcast_to(np.arange(NE, dtype=np.float32), (P, NE)),
        "c_token": np.arange(P, dtype=np.float32)[:, None] + P * np.arange(NT, dtype=np.float32)[None, :],
        "c_tile": np.arange(RT, dtype=np.float32)[None, :],
        "c_tri": np.triu(np.ones((P, P), np.float32), 1),
    }
    nc = bacc.Bacc("TRN2", target_bir_lowering=False, num_devices=1)
    arrays = {n: np.ascontiguousarray(v) for n, v in arrays.items()}
    args = {n: nc.dram_tensor("in_" + n, v.shape, mybir.dt.from_np(v.dtype), kind="ExternalInput").ap()
            for n, v in arrays.items()}
    out = nc.dram_tensor("out_0_dram", (N, HID), mybir.dt.float32, kind="ExternalOutput").ap()
    build(nc, B, T, HID, H, F, NE, TOPK, out=out, **args)
    r = run_bass_kernel_spmd(nc, [{"in_" + n: v for n, v in arrays.items()}], core_ids=[0])
    return r.results[0]["out_0_dram"].reshape(B, T, HID)
```
